# Optimizing a Trainium2 kernel written in Bass

```python
import numpy as np
import jax
import jax.numpy as jnp

def _softmax(x, axis=-1):
    return jax.nn.softmax(x, axis=axis)

def _gelu(x):
    return jax.nn.gelu(x, approximate=True)

def _silu(x):
    return jax.nn.silu(x)

def _sigmoid(x):
    return jax.nn.sigmoid(x)

def _layernorm(x, axis=-1, eps=1e-05):
    m = jnp.mean(x, axis=axis, keepdims=True)
    v = jnp.var(x, axis=axis, keepdims=True)
    return (x - m) / jnp.sqrt(v + eps)

def _scatter_add(tgt, idx, src, axis=0):
    return tgt.at[idx].add(src)

def _segment_sum(src, seg, n):
    return jax.ops.segment_sum(src, seg, n)
kernel_name = 'mk_macaron_d1_jaxref_r8_3c3bdf'

def setup_inputs(seed: int=0):
    np.random.seed(seed)
    _w = jnp.asarray

    def _L0_attn_setup():
        import jax, jax.numpy as jnp
        import numpy as np
        EMBED_DIM = 256
        NUM_HEADS = 32
        NUM_KV_HEADS = 8
        HEAD_DIM = EMBED_DIM // NUM_HEADS
        KV_REPEAT = NUM_HEADS // NUM_KV_HEADS
        ROPE_BASE = 10000.0

        def rotate_half(x):
            x_even = x[..., ::2]
            x_odd = x[..., 1::2]
            return jnp.stack((-x_odd, x_even), axis=-1).reshape(x.shape)

        def rope_cos_sin(seq_len, dtype, start_pos=0):
            inv_freq = 1.0 / ROPE_BASE ** (jnp.arange(0, HEAD_DIM, 2, dtype=jnp.float32) / HEAD_DIM)
            pos = jnp.arange(start_pos, start_pos + seq_len, dtype=jnp.float32)
            freqs = jnp.outer(pos, inv_freq)
            cos = jnp.repeat(jnp.cos(freqs), 2, axis=-1).astype(dtype)
            sin = jnp.repeat(jnp.sin(freqs), 2, axis=-1).astype(dtype)
            return (cos[None, None], sin[None, None])
        key = jax.random.key(seed)
        ks = jax.random.split(key, 5)
        s = 0.02
        x = jax.random.normal(ks[0], (2, 256, EMBED_DIM), dtype=jnp.float32)
        Wq = jax.random.normal(ks[1], (EMBED_DIM, EMBED_DIM), dtype=jnp.float32) * s
        Wk = jax.random.normal(ks[2], (EMBED_DIM, NUM_KV_HEADS * HEAD_DIM), dtype=jnp.float32) * s
        Wv = jax.random.normal(ks[3], (EMBED_DIM, NUM_KV_HEADS * HEAD_DIM), dtype=jnp.float32) * s
        Wo = jax.random.normal(ks[4], (EMBED_DIM, EMBED_DIM), dtype=jnp.float32) * s
        return {'x': x, 'Wq': Wq, 'bq': jnp.zeros((EMBED_DIM,), jnp.float32), 'Wk': Wk, 'bk': jnp.zeros((NUM_KV_HEADS * HEAD_DIM,), jnp.float32), 'Wv': Wv, 'bv': jnp.zeros((NUM_KV_HEADS * HEAD_DIM,), jnp.float32), 'Wo': Wo, 'bo': jnp.zeros((EMBED_DIM,), jnp.float32)}
    _L0_attn_in = _L0_attn_setup()

    def _L0_ffn_setup():
        import jax, jax.numpy as jnp
        import numpy as np
        TOP_K = 4

        def _silu_and_mul(gu):
            g, u = jnp.split(gu, 2, axis=-1)
            return jax.nn.silu(g) * u
        key = jax.random.key(seed)
        ks = jax.random.split(key, 7)
        H, E, I, Is = (256, 16, 176, 704)
        s = 0.02
        return {'hidden_states': jax.random.normal(ks[0], (4, 128, H), dtype=jnp.float32), 'gate_w': jax.random.normal(ks[1], (E, H), dtype=jnp.float32) * s, 'sgate_w': jax.random.normal(ks[2], (1, H), dtype=jnp.float32) * s, 'w13': jax.random.normal(ks[3], (E, 2 * I, H), dtype=jnp.float32) * s, 'w2': jax.random.normal(ks[4], (E, H, I), dtype=jnp.float32) * s, 'shared_gate_up_w': jax.random.normal(ks[5], (2 * Is, H), dtype=jnp.float32) * s, 'shared_down_w': jax.random.normal(ks[6], (H, Is), dtype=jnp.float32) * s}
    _L0_ffn_in = _L0_ffn_setup()
    _d = {'L0_attn_x': _L0_attn_in['x'], 'L0_attn_Wq': _L0_attn_in['Wq'], 'L0_attn_bq': _L0_attn_in['bq'], 'L0_attn_Wk': _L0_attn_in['Wk'], 'L0_attn_bk': _L0_attn_in['bk'], 'L0_attn_Wv': _L0_attn_in['Wv'], 'L0_attn_bv': _L0_attn_in['bv'], 'L0_attn_Wo': _L0_attn_in['Wo'], 'L0_attn_bo': _L0_attn_in['bo'], 'L0_ffn_gate_w': _L0_ffn_in['gate_w'], 'L0_ffn_sgate_w': _L0_ffn_in['sgate_w'], 'L0_ffn_w13': _L0_ffn_in['w13'], 'L0_ffn_w2': _L0_ffn_in['w2'], 'L0_ffn_shared_gate_up_w': _L0_ffn_in['shared_gate_up_w'], 'L0_ffn_shared_down_w': _L0_ffn_in['shared_down_w']}
    _x0 = _d['L0_attn_x']
    _d['L0_attn_x'] = jax.random.normal(jax.random.fold_in(jax.random.key(seed), 1), (1, 1024, 256), dtype=_x0.dtype)
    del _x0
    return _d

def reference(L0_attn_x, L0_attn_Wq, L0_attn_bq, L0_attn_Wk, L0_attn_bk, L0_attn_Wv, L0_attn_bv, L0_attn_Wo, L0_attn_bo, L0_ffn_gate_w, L0_ffn_sgate_w, L0_ffn_w13, L0_ffn_w2, L0_ffn_shared_gate_up_w, L0_ffn_shared_down_w):

    def _L0_attn_ref(x, Wq, bq, Wk, bk, Wv, bv, Wo, bo):
        import jax, jax.numpy as jnp
        import numpy as np
        EMBED_DIM = 256
        NUM_HEADS = 32
        NUM_KV_HEADS = 8
        HEAD_DIM = EMBED_DIM // NUM_HEADS
        KV_REPEAT = NUM_HEADS // NUM_KV_HEADS
        ROPE_BASE = 10000.0

        def rotate_half(x):
            x_even = x[..., ::2]
            x_odd = x[..., 1::2]
            return jnp.stack((-x_odd, x_even), axis=-1).reshape(x.shape)

        def rope_cos_sin(seq_len, dtype, start_pos=0):
            inv_freq = 1.0 / ROPE_BASE ** (jnp.arange(0, HEAD_DIM, 2, dtype=jnp.float32) / HEAD_DIM)
            pos = jnp.arange(start_pos, start_pos + seq_len, dtype=jnp.float32)
            freqs = jnp.outer(pos, inv_freq)
            cos = jnp.repeat(jnp.cos(freqs), 2, axis=-1).astype(dtype)
            sin = jnp.repeat(jnp.sin(freqs), 2, axis=-1).astype(dtype)
            return (cos[None, None], sin[None, None])
        B, T, C = x.shape
        q = (x @ Wq + bq).reshape(B, T, NUM_HEADS, HEAD_DIM).transpose(0, 2, 1, 3)
        k = (x @ Wk + bk).reshape(B, T, NUM_KV_HEADS, HEAD_DIM).transpose(0, 2, 1, 3)
        v = (x @ Wv + bv).reshape(B, T, NUM_KV_HEADS, HEAD_DIM).transpose(0, 2, 1, 3)
        cos, sin = rope_cos_sin(T, q.dtype, start_pos=0)
        q = q * cos + rotate_half(q) * sin
        k = k * cos + rotate_half(k) * sin
        k_rep = jnp.repeat(k, KV_REPEAT, axis=1)
        v_rep = jnp.repeat(v, KV_REPEAT, axis=1)
        scale = np.sqrt(HEAD_DIM).astype(np.float32)
        scores = jnp.einsum('bhqd,bhkd->bhqk', q, k_rep) / scale
        qpos = jnp.arange(T)[:, None]
        kpos = jnp.arange(T)[None, :]
        scores = jnp.where((kpos > qpos)[None, None], -jnp.inf, scores)
        attn = jax.nn.softmax(scores, axis=-1)
        out = jnp.einsum('bhqk,bhkd->bhqd', attn, v_rep)
        out = out.transpose(0, 2, 1, 3).reshape(B, T, C)
        return out @ Wo + bo

    def _L0_ffn_ref(hidden_states, gate_w, sgate_w, w13, w2, shared_gate_up_w, shared_down_w):
        import jax, jax.numpy as jnp
        import numpy as np
        TOP_K = 4

        def _silu_and_mul(gu):
            g, u = jnp.split(gu, 2, axis=-1)
            return jax.nn.silu(g) * u
        B, S, H = hidden_states.shape
        x = hidden_states.reshape(-1, H)
        E = gate_w.shape[0]
        shared = _silu_and_mul(x @ shared_gate_up_w.T) @ shared_down_w.T
        shared = shared * jax.nn.sigmoid(x @ sgate_w.T)
        router_logits = x @ gate_w.T
        routing_weights = jax.nn.softmax(router_logits.astype(jnp.float32), axis=-1)
        topk_w, topk_ids = jax.lax.top_k(routing_weights, TOP_K)

        def body(acc, ew):
            w13_e, w2_e, e = ew
            coef = jnp.sum(jnp.where(topk_ids == e, topk_w, 0.0), axis=-1)
            h = _silu_and_mul(x @ w13_e.T)
            acc = acc + (h @ w2_e.T).astype(jnp.float32) * coef[:, None]
            return (acc, None)
        init = jnp.zeros((x.shape[0], H), dtype=jnp.float32)
        sparse_out, _ = jax.lax.scan(body, init, (w13, w2, jnp.arange(E)))
        out = shared + sparse_out.astype(x.dtype)
        return out.reshape(B, S, H)
    x = L0_attn_x
    x = x + 0.5 * _L0_ffn_ref(_layernorm(x, axis=-1), L0_ffn_gate_w, L0_ffn_sgate_w, L0_ffn_w13, L0_ffn_w2, L0_ffn_shared_gate_up_w, L0_ffn_shared_down_w)
    x = x + _L0_attn_ref(_layernorm(x, axis=-1), L0_attn_Wq, L0_attn_bq, L0_attn_Wk, L0_attn_bk, L0_attn_Wv, L0_attn_bv, L0_attn_Wo, L0_attn_bo)
    x = x + 0.5 * _L0_ffn_ref(_layernorm(x, axis=-1), L0_ffn_gate_w, L0_ffn_sgate_w, L0_ffn_w13, L0_ffn_w2, L0_ffn_shared_gate_up_w, L0_ffn_shared_down_w)
    return x

_drawn_inputs = setup_inputs


def setup_inputs(seed=0):
    import zlib

    import numpy as np

    out = dict(_drawn_inputs(seed))
    spreads = {'L0_attn_bq': (0.0, 0.8),
     'L0_attn_bk': (0.0, 0.8),
     'L0_attn_bv': (0.0, 0.281),
     'L0_attn_bo': (0.0, 0.1)}
    factors = {'L0_attn_Wq': 8.0,
     'L0_attn_Wk': 8.0,
     'L0_attn_Wv': 5.797,
     'L0_ffn_gate_w': 8.0,
     'L0_ffn_sgate_w': 8.0,
     'L0_ffn_w13': 8.0,
     'L0_ffn_w2': 8.0,
     'L0_ffn_shared_gate_up_w': 4.028,
     'L0_ffn_shared_down_w': 4.031}
    for name, (base, spread) in spreads.items():
        noise = np.random.default_rng([zlib.crc32(name.encode()), seed]).standard_normal(out[name].shape)
        drawn = base * np.exp(spread * noise) if base else spread * noise
        out[name] = jnp.asarray(drawn.astype(out[name].dtype))
    for name, factor in factors.items():
        out[name] = (out[name] * factor).astype(out[name].dtype)
    return out
```

```python
import concourse.bass as bass
from concourse import mybir
from contextlib import ExitStack

F32, F16, BF16 = mybir.dt.float32, mybir.dt.float16, mybir.dt.bfloat16
ALU, ACT, AX = mybir.AluOpType, mybir.ActivationFunctionType, mybir.AxisListType

P = 128
T, D = 1024, 256
TT = T // P
KC = D // P
NE, FE, FS = 16, 176, 704
TOPK = 4
FEXP = NE * FE
MX = FEXP // P
MT = -(-(FEXP + FS) // P)
WC = 3 * D
NG = NE + 1
NC = 2
CH = T // NC
TPC = TT // NC
NH, NKV, HD = 32, 8, 8
GQ = NH // NKV
QW, KW = NH * HD, NKV * HD
QKV = QW + 2 * KW
ROW = 32
GLO = P // ROW
GHI = NKV // GLO
EPS = 1e-5
WS = 64.0
NEG = -1.0e30
SCALE = HD ** -0.5


def coefficient_spans():
    spans = []
    for m in range(MT):
        f0 = m * P
        if m < MX:
            e = f0 // FE
            cut = min(P, (e + 1) * FE - f0)
            nxt = e + 1
        else:
            e, cut, nxt = NE, P, NE
        if cut == P:
            cut, nxt = P // 2, e
        spans.append([(m, 0, cut, e), (m, cut, P - cut, nxt)])
    return spans


def attention_schedule():
    events, n, k = [], 0, 0

    def maxima(t):
        nonlocal k
        items = [("q1", t)]
        for h in range(NH):
            for kc in range(t // 4 + 1):
                items.append(("m", k, t, h, kc))
                k += 1
        return items + [("mx", t)]

    def projection(t):
        return [("f1", 2 * t), ("f1", 2 * t + 1), ("f2a", t), ("f2b", t), ("f3", t)]

    events += maxima(0) + [("q2", 0)]
    last = None
    for i in range(TT):
        steps = [(2 * i + g, g, kt) for g in range(GHI) for kt in range(i + 1)]
        back = maxima(i + 1) if i + 1 < TT else []
        if i:
            proj = projection(i - 1)
            if back:
                for q, item in enumerate(proj):
                    back.insert(1 + 6 * (q + 1), item)
            else:
                back = proj
        places = 3 * (len(steps) - 1)
        for s, (u, g, kt) in enumerate(steps):
            for place in range(3):
                if place < 2:
                    events.append(("st", n, place, u, g, kt, i))
                elif last is not None:
                    events.append(("pv",) + last)
                    if last[3] == last[4]:
                        events.append(("o", last[1]))
                at = 3 * s + place
                if at < places and not (i and at < 3):
                    lo = 3 if i else 0
                    share = [len(back) * (at - lo + d) // (places - lo) for d in (0, 1)]
                    events += back[share[0]:share[1]]
                if at == places and places - (3 if i else 0) <= 0:
                    events += back
            last = (n, u, g, kt, i)
            n += 1
        if i + 1 < TT:
            events.append(("q2", i + 1))
    events += [("pv",) + last, ("o", last[1])] + projection(TT - 1)
    return events


def build(nc, x_in, w_in, gate_in, qkvo_in, bias_in, rope_in, ident_in, mask_in, out, stages=3):
    ctx = ExitStack()
    with ctx:
        def sb(name, shape, dt):
            return ctx.enter_context(nc.sbuf_tensor(name, shape, dt))

        def sem(name):
            return ctx.enter_context(nc.semaphore(name))

        psum = ctx.enter_context(nc.psum_tensor("psum", [P, 8 * 512], F32))
        bank = [psum[:, 512 * i:512 * (i + 1)] for i in range(8)]
        coef_dram = [nc.dram_tensor(f"coef_dram{f}", (NG, T), F32).ap() for f in range(2)]

        x_res = sb("x_res", [P, TT, D], F32)
        xT = sb("xT", [P, 2, KC, T], F16)
        W_hi = sb("W_hi", [P, MT, WC], F16)
        W_lo = sb("W_lo", [P, MT, WC], F16)
        gate_f = sb("gate_f", [P, KC, NG], F32)
        gate_h = sb("gate_h", [P, 2, KC, NG], F16)
        qkvo_h = sb("qkvo_h", [P, 2, KC, QKV + D], F16)
        bias = sb("bias", [P, QKV + D], F32)
        rope = sb("rope", [P, 2, TT, HD], F32)
        ident = sb("ident", [P, P], F32)
        ident16 = sb("ident16", [P, P], F16)
        identb = sb("identb", [P, P], BF16)
        maskf = sb("maskf", [P, 2, P], F32)
        maskb = sb("maskb", [P, 2, P], BF16)
        w_stage = sb("w_stage", [P, 2, WC], F32)

        R1 = sb("R1", [P, 4096], F32)
        R2 = sb("R2", [P, 4096], F32)
        xn = R1[:, 0:2048].rearrange("p (t d) -> p t d", t=TT)
        x_hl = R1[:, 2048:4096].bitcast(F16).rearrange("p (a t d) -> p a t d", a=2, t=TT)
        v = R1[:, 0:2048].rearrange("p (s c n) -> p s c n", s=2, c=NC)
        hc = R1[:, 2048:3072].rearrange("p (c n) -> p c n", c=NC)
        sg = R1[:, 3072:4096].rearrange("p (c n) -> p c n", c=NC)
        hT = R2[:, 0:2048].bitcast(F16).rearrange("p (a s n) -> p a s n", a=2, s=2)
        C = R2[:, 2048:4096].rearrange("p (s n) -> p s n", s=2)
        qaug = R2[:, :].bitcast(F16).rearrange("p (t h r) -> p t h r", t=TT, r=ROW)
        prob = R1[:, :].rearrange("p (s g n) -> p s g n", s=2, g=GLO)
        kT = sb("kT", [P, NKV, T], F16)
        qkvo_f = kT[:, :, :].rearrange("p g n -> p (g n)").bitcast(F32)[:, 0:KC * (QKV + D)]\
            .rearrange("p (k n) -> p k n", k=KC)
        kaug = sb("kaug", [P, TT, NKV, ROW], F16)
        vals = sb("vals", [P, TT, NKV, 32], F32)
        qkv = sb("qkv", [P, 2, QKV], F32)
        rot_a = sb("rot_a", [P, 2, QW + KW], F32)
        rot_b = sb("rot_b", [P, QW + KW], F32)
        qT1 = sb("qT1", [P, 2, GHI * GQ, P], F16)
        qT2 = sb("qT2", [P, 2, GHI * GQ, P], F16)
        m_part = sb("m_part", [P, NH, 2], F32)
        m_row = sb("m_row", [P, NH], F32)
        oT = sb("oT", [P, 2, 512], F32)
        o_rs = sb("o_rs", [P, GQ, GLO], F32)
        o_tok = sb("o_tok", [P, D], F32)
        o_hl = sb("o_hl", [P, 2, D], F16)
        oTT = sb("oTT", [P, 2, KC, P], F16)
        st = sb("st", [P, TT, 6], F32)
        mv = sb("mv", [P, TT, 2], F32)
        sd = sb("sd", [P, TT], F32)
        rs = sb("rs", [P, TT], F32)
        lg = sb("lg", [P, TT, NG], F32)
        mx = sb("mx", [P, TT], F32)
        ex = sb("ex", [P, TT, NG], F32)
        den = sb("den", [P, TT, 2], F32)
        rden = sb("rden", [P, TT, 2], F32)
        pr = sb("pr", [P, TT, NE + TOPK], F32)
        top = sb("top", [P, TT, 8], F32)
        rest = sb("rest", [P, TT, NE + TOPK], F32)
        cf = sb("cf", [P, TT, NG], F32)
        cT = sb("cT", [NG, T], F32)

        s_x = [sem(f"s_x{t}") for t in range(TT)]
        s_const = sem("s_const")
        s_qkvo = sem("s_qkvo")
        s_w = [sem(f"s_w{i}") for i in range(2)]
        s_dve = sem("s_dve")
        s_pool = sem("s_pool")
        s_whi = sem("s_whi")
        s_wlo = sem("s_wlo")
        s_ghi = sem("s_ghi")
        s_glo = sem("s_glo")
        s_var = sem("s_var")
        s_sd = sem("s_sd")
        s_xn = sem("s_xn")
        s_xh = sem("s_xh")
        s_xl = sem("s_xl")
        s_xps = sem("s_xps")
        s_xT = sem("s_xT")
        s_lg = sem("s_lg")
        s_d = sem("s_d")
        s_ex = sem("s_ex")
        s_cf = sem("s_cf")
        s_cps = sem("s_cps")
        s_cT = sem("s_cT")
        s_cdram = sem("s_cdram")
        s_C = [sem(f"s_C{i}") for i in range(2)]
        s_gu = [sem(f"s_gu{c}") for c in range(NC)]
        s_sg = [sem(f"s_sg{c}") for c in range(NC)]
        s_v = [sem(f"s_v{c}") for c in range(NC)]
        s_hc = [sem(f"s_hc{c}") for c in range(NC)]
        s_hhi = [sem(f"s_hhi{c}") for c in range(NC)]
        s_hlo = [sem(f"s_hlo{c}") for c in range(NC)]
        s_y = [sem(f"s_y{c}") for c in range(NC)]
        s_res = sem("s_res")
        s_ident = sem("s_ident")
        s_out = sem("s_out")
        s_qkvo_h = sem("s_qkvo_h")
        s_qkvo_l = sem("s_qkvo_l")
        s_ready = sem("s_ready")
        s_xb = sem("s_xb")
        s_proj = sem("s_proj")
        s_qkv = sem("s_qkv")
        s_rot = sem("s_rot")
        s_qkhi = sem("s_qkhi")
        s_qklo = sem("s_qklo")
        s_kps = sem("s_kps")
        s_kT = sem("s_kT")
        s_bank7 = sem("s_bank7")
        s_free7 = sem("s_free7")
        s_s1 = sem("s_s1")
        s_max = sem("s_max")
        s_m = sem("s_m")
        s_st = sem("s_st")
        s_exp = sem("s_exp")
        s_pv = sem("s_pv")
        s_oT = sem("s_oT")
        s_ohi = sem("s_ohi")
        s_olo = sem("s_olo")
        N_CONST = 5 * 16
        events = attention_schedule()
        use7 = {e: n for n, e in enumerate(e for e in events if e[0] in ("q1", "q2", "f1", "f2b", "f3"))}
        unit_end = {e[2]: e[1] + 1 for e in events if e[0] == "pv"}
        max_count = {t: sum(e[0] == "m" and e[2] <= t for e in events) for t in range(TT)}

        block = ctx.enter_context(nc.Block())

        @block.sync
        def _(sp):
            xv = x_in.rearrange("(t p) d -> t p d", p=P)
            for t in range(TT):
                sp.dma_start(x_res[:, t, :], xv[t]).then_inc(s_x[t], 16)
            sp.dma_start(gate_f[:], gate_in).then_inc(s_const, 16)
            sp.dma_start(ident[:], ident_in).then_inc(s_const, 16)
            sp.dma_start(maskf[:], mask_in).then_inc(s_const, 16)
            sp.dma_start(bias[:], bias_in).then_inc(s_const, 16)
            sp.dma_start(rope[:], rope_in).then_inc(s_const, 16)
            sp.dma_start(qkvo_f, qkvo_in).then_inc(s_qkvo, 16)

            def coefficients(f):
                sp.wait_ge(s_cT, 2 * (f + 1))
                sp.dma_start(coef_dram[f], cT[:]).then_inc(s_cdram, 16)
                sp.wait_ge(s_cdram, 16 * (f + 1))
                for m, pair in enumerate(coefficient_spans()):
                    M = f * MT + m
                    if M >= 2:
                        sp.wait_ge(s_hc[0], M - 1)
                        sp.wait_ge(s_hc[1], M - 1)
                    for _, p0, n, e in pair:
                        sp.dma_start(C[p0:p0 + n, m % 2, :],
                                     coef_dram[f][e:e + 1, :].to_broadcast([n, T])).then_inc(s_C[m % 2], 16)

            coefficients(0)
            if stages == 3:
                coefficients(1)
            ov = out.rearrange("(t p) d -> p t d", p=P)
            for b in range(4):
                sp.wait_ge(s_res, {1: b + 1, 2: 4, 3: 4 + b + 1}[stages])
                if stages == 2:
                    sp.wait_ge(s_free7, use7[('f3', 2 * b + 1)] + 1)
                sp.dma_start(ov[:, 2 * b:2 * b + 2, :], x_res[:, 2 * b:2 * b + 2, :]).then_inc(s_out, 16)
            sp.wait_ge(s_out, 64)

        @block.gpsimd
        def _(pool):
            def weighted(f, m, j, c):
                M = f * MT + m
                pool.wait_ge(s_v[c], M + 1)
                pool.wait_ge(s_C[j], 32 * (M // 2 + 1) if isinstance(M, int) else 16 * (M - j) + 32)
                if not isinstance(M, int) or M >= 1:
                    pool.wait_ge(s_hlo[c], M)
                nc.gpsimd.tensor_tensor(hc[:, c, :], v[:, j, c, :], C[:, j, c * CH:(c + 1) * CH],
                                        ALU.mult).then_inc(s_hc[c], 1)

            def constants():
                pool.wait_ge(s_qkvo_l, 1)
                nc.gpsimd.memset(kT[:, :, :].rearrange("p g n -> p (g n)").bitcast(F32), 0.0)
                nc.gpsimd.memset(kaug[:], 0.0)
                nc.gpsimd.memset(vals[:], 0.0).then_inc(s_pool, 1)
                pool.wait_ge(s_pool, 1)
                nc.gpsimd.memset(kaug[:, :, :, 24:26], 1.0)
                nc.gpsimd.memset(vals[:, :, :, HD:HD + 1], 1.0).then_inc(s_ready, 1)

            def ffn(f, between=None):
                def step(s, j):
                    for c in range(NC):
                        weighted(f, s - 1, 1 - j, c)
                step(1, 1)
                step(2, 0)
                if between:
                    between()
                step(3, 1)
                with pool.Fori(2, MT // 2 - 1) as i:
                    step(2 * i, 0)
                    step(2 * i + 1, 1)
                step(MT - 2, 0)
                step(MT - 1, 1)
                for c in range(NC):
                    weighted(f, MT - 1, 1, c)

            ffn(0, constants)
            if stages == 1:
                return
            for c in range(NC):
                pool.wait_ge(s_y[c], MT)
            nc.gpsimd.memset(qaug[:, :, :, 24:32], 0.0).then_inc(s_ready, 1)
            for t in range(TT):
                pool.wait_ge(s_qkv, t + 1)
                if t >= 2:
                    pool.wait_ge(s_qklo, t - 1)
                x = qkv[:, t % 2, 0:QW + KW].rearrange("p (h n e) -> p h n e", n=HD // 2, e=2)
                cos = rope[:, 0, t, :].unsqueeze(1).to_broadcast([P, NH + NKV, HD])
                sin = rope[:, 1, t, :].rearrange("p (n e) -> p n e", e=2).unsqueeze(1)\
                    .to_broadcast([P, NH + NKV, HD // 2, 2])
                ra = rot_a[:, t % 2, :]
                nc.gpsimd.tensor_tensor(ra.rearrange("p (h d) -> p h d", d=HD),
                                        qkv[:, t % 2, 0:QW + KW].rearrange("p (h d) -> p h d", d=HD),
                                        cos, ALU.mult)
                nc.gpsimd.tensor_tensor(rot_b[:].rearrange("p (h n e) -> p h n e", n=HD // 2, e=2),
                                        x[:, :, :, ::-1], sin, ALU.mult).then_inc(s_pool, 1)
                pool.wait_ge(s_pool, 2 + t)
                nc.gpsimd.tensor_tensor(ra, ra, rot_b[:], ALU.add).then_inc(s_rot, 1)
                pool.wait_ge(s_rot, t + 1)
                if t == 0:
                    pool.wait_ge(s_xn, 2 * TT)
                nc.gpsimd.tensor_tensor(x_res[:, t, :], x_res[:, t, :], bias[:, QKV:QKV + D],
                                        ALU.add).then_inc(s_xb, 1)
                pool.wait_ge(s_xb, t + 1)
            if stages == 3:
                ffn(1)

        @block.scalar
        def _(act):
            def load_weights(m, j):
                if not isinstance(m, int) or m >= 2:
                    act.wait_ge(s_wlo, m - 1)
                src = w_in[m] if isinstance(m, int) else w_in[bass.ds(m, 1), :, :].rearrange("o p n -> p (o n)")
                act.dma_start(w_stage[:, j, :], src).then_inc(s_w[j], 16)

            def weights_high(m, j):
                act.wait_ge(s_w[j], 16 * (m // 2 + 1) if isinstance(m, int) else 8 * (m - j) + 16)
                nc.scalar.activation(W_hi[:, m, :], w_stage[:, j, :], ACT.Copy, scale=WS).then_inc(s_whi, 1)

            def layer_norm(r):
                act.wait_ge(s_var, r + 1)
                nc.scalar.activation(sd[:], mv[:, :, 1], ACT.Sqrt).then_inc(s_sd, 1)

                def evacuate(t):
                    act.wait_ge(s_xps, r * TT + t + 1)
                    ps = bank[4 + t % 2][:, 0:256].bitcast(F16).rearrange("p (a k n) -> p a k n", a=2, k=KC)
                    nc.scalar.activation(xT[:, :, :, t * P:(t + 1) * P], ps, ACT.Copy).then_inc(s_xT, 1)

                for t in range(TT):
                    act.wait_ge(s_xn, r * TT + t + 1)
                    nc.scalar.activation(x_hl[:, 0, t, :], xn[:, t, :], ACT.Copy).then_inc(s_xh, 1)
                    if t >= 1:
                        evacuate(t - 1)
                evacuate(TT - 1)

            def silu(f, m, c):
                M = f * MT + m
                act.wait_ge(s_gu[c], M + 1)
                if not isinstance(M, int) or M >= 1:
                    act.wait_ge(s_v[c], M)
                nc.scalar.activation(sg[:, c, :], bank[c][:, :], ACT.Silu, scale=1.0 / WS).then_inc(s_sg[c], 1)

            def high(f, m, j, c):
                M = f * MT + m
                act.wait_ge(s_hc[c], M + 1)
                if not isinstance(M, int) or M >= 2:
                    act.wait_ge(s_y[c], M - 1)
                nc.scalar.activation(hT[:, 0, j, c * CH:(c + 1) * CH], hc[:, c, :], ACT.Copy).then_inc(s_hhi[c], 1)

            def ffn(f):
                act.wait_ge(s_d, f + 1)
                nc.scalar.activation(ex[:], lg[:], ACT.Exp).then_inc(s_ex, 1)

                def step(s, j):
                    if f == 0 and (not isinstance(s, int) or s + 2 < MT):
                        load_weights(s + 2, j)
                    if f == 0 and (not isinstance(s, int) or s + 1 < MT):
                        weights_high(s + 1, 1 - j)
                    for c in range(NC):
                        silu(f, s, c)
                        if not isinstance(s, int) or s >= 2:
                            high(f, s - 1, 1 - j, c)
                step(0, 0)
                step(1, 1)
                for h in range(2):
                    act.wait_ge(s_cps, 2 * f + h + 1)
                    nc.scalar.activation(cT[:, h * 512:(h + 1) * 512], bank[7 - h][0:NG, :],
                                         ACT.Copy).then_inc(s_cT, 1)
                for c in range(NC):
                    high(f, 0, 0, c)
                step(2, 0)
                step(3, 1)
                with act.Fori(2, MT // 2 - 1) as i:
                    step(2 * i, 0)
                    step(2 * i + 1, 1)
                step(MT - 2, 0)
                step(MT - 1, 1)
                for c in range(NC):
                    high(f, MT - 1, 1, c)

            load_weights(0, 0)
            load_weights(1, 1)
            act.wait_ge(s_const, N_CONST)
            nc.scalar.activation(gate_h[:, 0], gate_f[:], ACT.Copy, scale=WS).then_inc(s_ghi, 1)
            weights_high(0, 0)
            layer_norm(0)
            act.wait_ge(s_qkvo, 16)
            nc.scalar.activation(qkvo_h[:, 0], qkvo_f, ACT.Copy, scale=WS).then_inc(s_qkvo_h, 1)
            ffn(0)
            if stages == 1:
                return
            layer_norm(1)

            def keys(t):
                act.wait_ge(s_kps, t + 1)
                ps = bank[2 + t % 2][:, 0:P].bitcast(F16).rearrange("p (a n) -> p a n", a=GHI)
                for g in range(GLO):
                    rows = slice(ROW * g, ROW * (g + 1))
                    ins = nc.scalar.activation(kT[rows, g:NKV:GLO, t * P:(t + 1) * P], ps[rows], ACT.Copy)
                ins.then_inc(s_kT, 1)

            for t in range(TT):
                act.wait_ge(s_rot, t + 1)
                if t == 0:
                    act.wait_ge(s_ready, 2)
                q = rot_a[:, t % 2, 0:QW].rearrange("p (h d) -> p h d", d=HD).unsqueeze(2)
                k = rot_a[:, t % 2, QW:QW + KW].rearrange("p (h d) -> p h d", d=HD).unsqueeze(2)
                nc.scalar.activation(qaug[:, t].rearrange("p h (a d) -> p h a d", d=HD)[:, :, 0:4:2, :],
                                     q.to_broadcast([P, NH, 2, HD]), ACT.Copy)
                nc.scalar.activation(kaug[:, t].rearrange("p h (a d) -> p h a d", d=HD)[:, :, 0:2, :],
                                     k.to_broadcast([P, NKV, 2, HD]), ACT.Copy).then_inc(s_qkhi, 1)
                if t >= 1:
                    keys(t - 1)
            keys(TT - 1)

            for e in events:
                if e[0] in ("q1", "q2"):
                    act.wait_ge(s_bank7, use7[e] + 1)
                    dst = qT1 if e[0] == "q1" else qT2
                    nc.scalar.activation(dst[:, e[1] % 2].rearrange("p a n -> p (a n)"), bank[7].bitcast(F16),
                                         ACT.Copy).then_inc(s_free7, 1)
                elif e[0] == "st":
                    n, pair = e[1], e[2]
                    act.wait_ge(s_st, 2 * n + pair + 1)
                    if n >= 2:
                        act.wait_ge(s_pv, n - 1)
                    nc.scalar.activation(prob[:, n % 2, 2 * pair:2 * pair + 2, :].rearrange("p g n -> p (g n)"),
                                         psum[:, 1024 * pair:1024 * (pair + 1)], ACT.Exp,
                                         scale=SCALE).then_inc(s_exp, 1)
                elif e[0] == "o":
                    u = e[1]
                    act.wait_ge(s_pv, unit_end[u])
                    if u >= 2:
                        act.wait_ge(s_free7, use7[("f1", u - 2)] + 1)
                    nc.scalar.activation(oT[:, u % 2, :], bank[6], ACT.Copy).then_inc(s_oT, 1)
                elif e[0] == "f2a":
                    t = e[1]
                    act.wait_ge(s_free7, use7[("f1", 2 * t + 1)] + 1)
                    nc.scalar.activation(o_hl[:, 0], o_tok[:], ACT.Copy).then_inc(s_ohi, 1)
                elif e[0] == "f2b":
                    act.wait_ge(s_bank7, use7[e] + 1)
                    nc.scalar.activation(oTT[:, :, :, :].rearrange("p a k n -> p (a k n)"),
                                         bank[7][:, 0:256].bitcast(F16), ACT.Copy).then_inc(s_free7, 1)
            if stages == 3:
                layer_norm(2)
                ffn(1)

        @block.vector
        def _(dve):
            chain = [0]

            def link(ins):
                chain[0] += 1
                ins.then_inc(s_dve, 1)
                dve.wait_ge(s_dve, chain[0])

            def layer_norm(r):
                for t in range(TT):
                    if r == 0:
                        dve.wait_ge(s_x[t], 16)
                    elif r == 1:
                        dve.wait_ge(s_res, t // 2 + 1)
                    else:
                        dve.wait_ge(s_free7, use7[("f3", t)] + 1)
                    ins = nc.vector.bn_stats(st[:, t, :], x_res[:, t, :])
                link(ins)
                for t in range(TT):
                    ins = nc.vector.bn_aggr(mv[:, t, :], st[:, t, :])
                link(ins)
                nc.vector.tensor_scalar(mv[:, :, 1], mv[:, :, 1], EPS, None, ALU.add).then_inc(s_var, 1)
                dve.wait_ge(s_sd, r + 1)
                link(nc.vector.reciprocal(rs[:], sd[:]))

                def low(t):
                    dve.wait_ge(s_xh, r * TT + t + 1)
                    nc.vector.tensor_tensor(x_hl[:, 1, t, :], xn[:, t, :], x_hl[:, 0, t, :],
                                            ALU.subtract).then_inc(s_xl, 1)

                for t in range(TT):
                    nc.vector.tensor_scalar(xn[:, t, :], x_res[:, t, :], mv[:, t, 0:1], rs[:, t:t + 1],
                                            ALU.subtract, ALU.mult).then_inc(s_xn, 1)
                    if t >= 1:
                        low(t - 1)
                low(TT - 1)

            def router(f):
                dve.wait_ge(s_lg, f + 1)
                link(nc.vector.tensor_scalar(lg[:], bank[6][:, 0:TT * NG].rearrange("p (t e) -> p t e", t=TT),
                                             1.0 / WS, None, ALU.mult))
                link(nc.vector.tensor_reduce(mx[:], lg[:, :, 0:NE], axis=AX.X, op=ALU.max))
                nc.vector.tensor_tensor(lg[:, :, 0:NE], lg[:, :, 0:NE],
                                        mx[:, :].unsqueeze(2).to_broadcast([P, TT, NE]), ALU.subtract)
                nc.vector.tensor_scalar(lg[:, :, NE:NG], lg[:, :, NE:NG], -1.0, None, ALU.mult).then_inc(s_d, 1)
                dve.wait_ge(s_ex, f + 1)
                nc.vector.tensor_reduce(den[:, :, 0:1], ex[:, :, 0:NE], axis=AX.X, op=ALU.add)
                link(nc.vector.tensor_scalar(den[:, :, 1:2], ex[:, :, NE:NG], 1.0, None, ALU.add))
                link(nc.vector.reciprocal(rden[:], den[:]))
                nc.vector.tensor_tensor(pr[:, :, 0:NE], ex[:, :, 0:NE],
                                        rden[:, :, 0:1].to_broadcast([P, TT, NE]), ALU.mult)
                link(nc.vector.tensor_copy(cf[:, :, NE:NG], rden[:, :, 1:2]))
                for t in range(TT):
                    ins = nc.vector.max(top[:, t, :], pr[:, t, :])
                link(ins)
                link(nc.vector.memset(top[:, :, TOPK:8], -1.0))
                for t in range(TT):
                    ins = nc.vector.match_replace(out=rest[:, t, :], in_to_replace=top[:, t, :],
                                                  in_values=pr[:, t, :], imm_value=0.0)
                link(ins)
                nc.vector.tensor_tensor(cf[:, :, 0:NE], pr[:, :, 0:NE], rest[:, :, 0:NE],
                                        ALU.subtract).then_inc(s_cf, 1)

            def weights_low(m, j):
                dve.wait_ge(s_whi, m + 1)
                nc.vector.scalar_tensor_tensor(out=W_lo[:, m, :], in0=w_stage[:, j, :], scalar=WS,
                                               in1=W_hi[:, m, :], op0=ALU.mult,
                                               op1=ALU.subtract).then_inc(s_wlo, 1)

            def gated(f, m, j, c):
                M = f * MT + m
                dve.wait_ge(s_sg[c], M + 1)
                if not isinstance(M, int) or M >= 2:
                    dve.wait_ge(s_hc[c], M - 1)
                nc.vector.scalar_tensor_tensor(out=v[:, j, c, :], in0=bank[2 + c][:, :], scalar=1.0 / WS,
                                               in1=sg[:, c, :], op0=ALU.mult, op1=ALU.mult).then_inc(s_v[c], 1)

            def low(f, m, j, c):
                M = f * MT + m
                dve.wait_ge(s_hhi[c], M + 1)
                nc.vector.tensor_tensor(hT[:, 1, j, c * CH:(c + 1) * CH], hc[:, c, :],
                                        hT[:, 0, j, c * CH:(c + 1) * CH], ALU.subtract).then_inc(s_hlo[c], 1)

            def ffn(f):
                router(f)

                def step(s, j):
                    if f == 0 and (not isinstance(s, int) or s + 1 < MT):
                        weights_low(s + 1, 1 - j)
                    for c in range(NC):
                        gated(f, s, j, c)
                        if not isinstance(s, int) or s >= 2:
                            low(f, s - 1, 1 - j, c)
                step(0, 0)
                step(1, 1)
                if f == 0:
                    dve.wait_ge(s_qkvo_h, 1)
                    nc.vector.scalar_tensor_tensor(out=qkvo_h[:, 1], in0=qkvo_f, scalar=WS, in1=qkvo_h[:, 0],
                                                   op0=ALU.mult, op1=ALU.subtract).then_inc(s_qkvo_l, 1)
                for c in range(NC):
                    low(f, 0, 0, c)
                step(2, 0)
                step(3, 1)
                with dve.Fori(2, MT // 2 - 1) as i:
                    step(2 * i, 0)
                    step(2 * i + 1, 1)
                step(MT - 2, 0)
                step(MT - 1, 1)
                for c in range(NC):
                    low(f, MT - 1, 1, c)
                for b in range(4):
                    dve.wait_ge(s_y[b // 2], (f + 1) * MT)
                    xr = x_res[:, 2 * b:2 * b + 2, :]
                    nc.vector.scalar_tensor_tensor(out=xr, in0=bank[4 + b][:, :].rearrange("p (t d) -> p t d", t=2),
                                                   scalar=0.5 / WS, in1=xr, op0=ALU.mult,
                                                   op1=ALU.add).then_inc(s_res, 1)

            dve.wait_ge(s_const, N_CONST)
            nc.vector.tensor_copy(ident16[:], ident[:])
            nc.vector.tensor_copy(identb[:], ident[:])
            nc.vector.memset(pr[:, :, NE:NE + TOPK], -1.0)
            nc.vector.tensor_copy(maskb[:], maskf[:]).then_inc(s_ident, 1)
            layer_norm(0)
            dve.wait_ge(s_ghi, 1)
            nc.vector.scalar_tensor_tensor(out=gate_h[:, 1], in0=gate_f[:], scalar=WS, in1=gate_h[:, 0],
                                           op0=ALU.mult, op1=ALU.subtract).then_inc(s_glo, 1)
            weights_low(0, 0)
            ffn(0)
            if stages == 1:
                return
            layer_norm(1)

            def split_low(t):
                dve.wait_ge(s_qkhi, t + 1)
                q = rot_a[:, t % 2, 0:QW].rearrange("p (h d) -> p h d", d=HD)
                k = rot_a[:, t % 2, QW:QW + KW].rearrange("p (h d) -> p h d", d=HD)
                nc.vector.tensor_tensor(qaug[:, t, :, HD:2 * HD], q, qaug[:, t, :, 0:HD], ALU.subtract)
                nc.vector.tensor_tensor(kaug[:, t, :, 2 * HD:3 * HD], k, kaug[:, t, :, 0:HD],
                                        ALU.subtract).then_inc(s_qklo, 1)

            for t in range(TT):
                dve.wait_ge(s_proj, t + 1)
                if t >= 2:
                    dve.wait_ge(s_rot, t - 1)
                nc.vector.scalar_tensor_tensor(out=qkv[:, t % 2, :], in0=bank[t % 2][:, 0:QKV], scalar=1.0 / WS,
                                               in1=bias[:, 0:QKV], op0=ALU.mult, op1=ALU.add).then_inc(s_qkv, 1)
                dve.wait_ge(s_qkv, t + 1)
                nc.vector.tensor_copy(vals[:, t, :, 0:HD],
                                      qkv[:, t % 2, QW + KW:QKV].rearrange("p (h d) -> p h d", d=HD))
                if t >= 1:
                    split_low(t - 1)
            split_low(TT - 1)

            for e in events:
                if e[0] == "m":
                    _, k, t, h, kc = e
                    dve.wait_ge(s_s1, k + 1)
                    n = min(4, t + 1 - 4 * kc) * P
                    nc.vector.tensor_reduce(m_part[:, h, kc:kc + 1], bank[4 + k % 2][:, 0:n], axis=AX.X,
                                            op=ALU.max).then_inc(s_max, 1)
                elif e[0] == "mx":
                    t = e[1]
                    dve.wait_ge(s_max, max_count[t])
                    if t >= 4:
                        link(nc.vector.tensor_tensor(m_row[:], m_part[:, :, 0], m_part[:, :, 1], ALU.max))
                    else:
                        link(nc.vector.tensor_copy(m_row[:], m_part[:, :, 0]))
                    link(nc.vector.tensor_scalar(qaug[:, t, :, 24], m_row[:], -1.0, None, ALU.mult))
                    nc.vector.scalar_tensor_tensor(out=qaug[:, t, :, 25], in0=m_row[:], scalar=-1.0,
                                                   in1=qaug[:, t, :, 24], op0=ALU.mult,
                                                   op1=ALU.subtract).then_inc(s_m, 1)
                    dve.wait_ge(s_m, t + 1)
                elif e[0] == "f1":
                    u = e[1]
                    dve.wait_ge(s_bank7, use7[e] + 1)
                    ps = bank[7].rearrange("p (j g r) -> p j g r", j=GQ, g=GLO)
                    link(nc.vector.reciprocal(o_rs[:], ps[:, :, :, HD]))
                    if u % 2 == 0 and u >= 2:
                        dve.wait_ge(s_olo, u // 2)
                    o = o_tok[:, (u % 2) * P:(u % 2 + 1) * P].rearrange("p (g j d) -> p j g d", g=GLO, j=GQ)
                    nc.vector.tensor_tensor(o, ps[:, :, :, 0:HD],
                                            o_rs[:, :, :].unsqueeze(3).to_broadcast([P, GQ, GLO, HD]),
                                            ALU.mult).then_inc(s_free7, 1)
                elif e[0] == "f2a":
                    dve.wait_ge(s_ohi, e[1] + 1)
                    nc.vector.tensor_tensor(o_hl[:, 1], o_tok[:], o_hl[:, 0], ALU.subtract).then_inc(s_olo, 1)
                elif e[0] == "f3":
                    t = e[1]
                    dve.wait_ge(s_bank7, use7[e] + 1)
                    dve.wait_ge(s_xb, t + 1)
                    nc.vector.scalar_tensor_tensor(out=x_res[:, t, :], in0=bank[7][:, 0:D], scalar=1.0 / WS,
                                                   in1=x_res[:, t, :], op0=ALU.mult,
                                                   op1=ALU.add).then_inc(s_free7, 1)
            if stages == 3:
                layer_norm(2)
                ffn(1)

        @block.tensor
        def _(pe):
            def split_product(o, stat, mov, k_parts, first=True, last=True, **kw):
                n = 0
                for k in range(k_parts):
                    for a, b in ((0, 0), (0, 1), (1, 0)):
                        ins = nc.tensor.matmul(o, stat(a, k), mov(b, k), start=first and n == 0,
                                               stop=last and n == 3 * k_parts - 1, **kw)
                        n += 1
                return ins

            def layer_norm(r):
                for t in range(TT):
                    pe.wait_ge(s_xl, r * TT + t + 1)
                    if t >= 2:
                        pe.wait_ge(s_xT, r * TT + t - 1)
                    ps = bank[4 + t % 2][:, 0:256].bitcast(F16)
                    for a in range(2):
                        for k in range(KC):
                            q = a * KC + k
                            ins = nc.tensor.transpose(ps[:, q * P:(q + 1) * P],
                                                      x_hl[:, a, t, k * P:(k + 1) * P], ident16[:])
                    ins.then_inc(s_xps, 1)

            def gate_up(f, m, c):
                M = f * MT + m
                if f == 0:
                    pe.wait_ge(s_wlo, m + 1)
                if not isinstance(M, int) or M >= 1:
                    pe.wait_ge(s_v[c], M)
                parts = (W_hi, W_lo)
                for u in range(2):
                    ins = split_product(
                        bank[2 * u + c][:, :],
                        lambda a, k: parts[a][:, m, (2 * u + k) * P:(2 * u + k + 1) * P],
                        lambda b, k: xT[:, b, k, c * CH:(c + 1) * CH], KC)
                ins.then_inc(s_gu[c], 1)

            def down(f, m, j, c, first=False, last=False):
                M = f * MT + m
                pe.wait_ge(s_hlo[c], M + 1)
                parts = (W_hi, W_lo)
                for t in range(c * TPC, (c + 1) * TPC):
                    o = bank[4 + t // 2][:, (t % 2) * D:(t % 2 + 1) * D]
                    ins = split_product(o, lambda a, k: hT[:, a, j, t * P:(t + 1) * P],
                                        lambda b, k: parts[b][:, m, 2 * D:3 * D], 1,
                                        first=first and t % 2 == 0, last=last, skip_group_check=True)
                ins.then_inc(s_y[c], 1)

            def ffn(f):
                for t in range(TT):
                    pe.wait_ge(s_xT, f * 2 * TT + t + 1)
                    if f == 0 and t == 0:
                        pe.wait_ge(s_glo, 1)
                    ins = split_product(bank[6][:, t * NG:(t + 1) * NG],
                                        lambda a, k: xT[:, a, k, t * P:(t + 1) * P],
                                        lambda b, k: gate_h[:, b, k, :], KC)
                ins.then_inc(s_lg, 1)

                def step(s, j, **kw):
                    for c in range(NC):
                        gate_up(f, s, c)
                        if not isinstance(s, int) or s >= 2:
                            down(f, s - 2, j, c, **kw)
                step(0, 0)
                step(1, 1)
                pe.wait_ge(s_cf, f + 1)
                for t in range(TT):
                    ins = nc.tensor.transpose(bank[7 - t // 4][0:NG, (t % 4) * P:(t % 4 + 1) * P],
                                              cf[:, t, :], ident[:])
                    if t % 4 == 3:
                        ins.then_inc(s_cps, 1)
                for c in range(NC):
                    gate_up(f, 2, c)
                    if c == 0:
                        pe.wait_ge(s_cT, 2 * (f + 1))
                    down(f, 0, 0, c, first=True)
                step(3, 1)
                with pe.Fori(2, MT // 2 - 1) as i:
                    step(2 * i, 0)
                    step(2 * i + 1, 1)
                step(MT - 2, 0)
                step(MT - 1, 1)
                for c in range(NC):
                    down(f, MT - 2, 0, c)
                for c in range(NC):
                    down(f, MT - 1, 1, c, last=True)

            pe.wait_ge(s_ident, 1)
            layer_norm(0)
            ffn(0)
            if stages == 1:
                return
            layer_norm(1)

            def keys(t):
                pe.wait_ge(s_qklo, t + 1)
                if t >= 2:
                    pe.wait_ge(s_kT, t - 1)
                ps = bank[2 + t % 2][:, 0:P].bitcast(F16)
                for a in range(GHI):
                    ins = nc.tensor.transpose(ps[:, a * P:(a + 1) * P],
                                              kaug[:, t, GLO * a:GLO * (a + 1), :].rearrange("p h r -> p (h r)"),
                                              ident16[:])
                ins.then_inc(s_kps, 1)

            pe.wait_ge(s_ready, 1)
            for t in range(TT):
                pe.wait_ge(s_xT, TT + t + 1)
                if t >= 2:
                    pe.wait_ge(s_qkv, t - 1)
                split_product(bank[t % 2][:, 0:QKV], lambda a, k: xT[:, a, k, t * P:(t + 1) * P],
                              lambda b, k: qkvo_h[:, b, k, 0:QKV], KC).then_inc(s_proj, 1)
                if t >= 1:
                    keys(t - 1)
            keys(TT - 1)

            for e in events:
                if e in use7 and use7[e] >= 1:
                    pe.wait_ge(s_free7, use7[e])
                if e[0] in ("q1", "q2"):
                    t = e[1]
                    if e[0] == "q2":
                        pe.wait_ge(s_m, t + 1)
                    elif t == 0:
                        pe.wait_ge(s_kT, TT)
                    ps = bank[7].bitcast(F16)
                    for a in range(GHI):
                        for j in range(GQ):
                            q = a * GQ + j
                            ins = nc.tensor.transpose(ps[:, q * P:(q + 1) * P],
                                                      qaug[:, t, GLO * q:GLO * (q + 1), :].rearrange("p h r -> p (h r)"),
                                                      ident16[:])
                    ins.then_inc(s_bank7, 1)
                elif e[0] == "m":
                    _, k, t, h, kc = e
                    if (h, kc) == (0, 0):
                        pe.wait_ge(s_free7, use7[("q1", t)] + 1)
                    if k >= 2:
                        pe.wait_ge(s_max, k - 1)
                    g = h // (GQ * GLO) * GLO + h % GLO
                    n = min(4, t + 1 - 4 * kc) * P
                    diag = kc == t // 4
                    if diag:
                        nc.tensor.matmul(bank[4 + k % 2][:, n - P:n], identb[:], maskb[:, 0, :],
                                         start=True, stop=False, skip_group_check=True)
                    nc.tensor.matmul(bank[4 + k % 2][:, 0:n], qT1[:, t % 2, h // GLO, :],
                                     kT[:, g, kc * 512:kc * 512 + n], start=not diag, stop=True,
                                     skip_group_check=diag).then_inc(s_s1, 1)
                elif e[0] == "st":
                    _, n, pair, u, gh, kt, t = e
                    if n >= 1:
                        pe.wait_ge(s_exp, 2 * (n - 1) + pair + 1)
                    if kt == 0 and pair == 0:
                        pe.wait_ge(s_free7, use7[("q2", t)] + 1)
                    for gl in (2 * pair, 2 * pair + 1):
                        ins = nc.tensor.matmul(bank[gl], kT[:, gh * GLO + gl, kt * P:(kt + 1) * P],
                                               qT2[:, t % 2, gh * GQ:(gh + 1) * GQ, :], start=True, stop=kt != t)
                        if kt == t:
                            ins = nc.tensor.matmul(bank[gl].rearrange("p (j n) -> p j n", j=GQ), identb[:],
                                                   maskb[:, 1, :].unsqueeze(1).to_broadcast([P, GQ, P]),
                                                   start=False, stop=True)
                    ins.then_inc(s_st, 1)
                elif e[0] == "pv":
                    _, n, u, gh, kt, t = e
                    pe.wait_ge(s_exp, 2 * n + 2)
                    if kt == 0 and u >= 1:
                        pe.wait_ge(s_oT, u)
                    for gl in range(GLO):
                        ins = nc.tensor.matmul(bank[6][32 * gl:32 * (gl + 1), :], vals[:, kt, gh * GLO + gl, :],
                                               prob[:, n % 2, gl, :], start=kt == 0, stop=kt == t)
                    ins.then_inc(s_pv, 1)
                elif e[0] == "f1":
                    u = e[1]
                    pe.wait_ge(s_oT, u + 1)
                    for j in range(GQ):
                        ins = nc.tensor.transpose(bank[7][:, j * P:(j + 1) * P], oT[:, u % 2, j * P:(j + 1) * P],
                                                  ident[:])
                    ins.then_inc(s_bank7, 1)
                elif e[0] == "f2b":
                    pe.wait_ge(s_olo, e[1] + 1)
                    ps = bank[7][:, 0:256].bitcast(F16)
                    for a in range(2):
                        for k in range(KC):
                            q = a * KC + k
                            ins = nc.tensor.transpose(ps[:, q * P:(q + 1) * P], o_hl[:, a, k * P:(k + 1) * P],
                                                      ident16[:])
                    ins.then_inc(s_bank7, 1)
                elif e[0] == "f3":
                    pe.wait_ge(s_free7, use7[("f2b", e[1])] + 1)
                    split_product(bank[7][:, 0:D], lambda a, k: oTT[:, a, k, :],
                                  lambda b, k: qkvo_h[:, b, k, QKV:QKV + D], KC).then_inc(s_bank7, 1)
            if stages == 3:
                layer_norm(2)
                ffn(1)


def kernel(L0_attn_x, L0_attn_Wq, L0_attn_bq, L0_attn_Wk, L0_attn_bk, L0_attn_Wv, L0_attn_bv, L0_attn_Wo,
           L0_attn_bo, L0_ffn_gate_w, L0_ffn_sgate_w, L0_ffn_w13, L0_ffn_w2, L0_ffn_shared_gate_up_w,
           L0_ffn_shared_down_w, stages=3):
    import numpy as np
    import concourse.bacc as bacc
    from concourse.bass_utils import run_bass_kernel_spmd

    nc, arrays, shape = program_and_arrays(np, bacc, L0_attn_x, L0_attn_Wq, L0_attn_bq, L0_attn_Wk, L0_attn_bk,
                                           L0_attn_Wv, L0_attn_bv, L0_attn_Wo, L0_attn_bo, L0_ffn_gate_w,
                                           L0_ffn_sgate_w, L0_ffn_w13, L0_ffn_w2, L0_ffn_shared_gate_up_w,
                                           L0_ffn_shared_down_w, stages)
    r = run_bass_kernel_spmd(nc, [arrays], core_ids=[0])
    return r.results[0]["out_dram"].reshape(shape)


def program_and_arrays(np, bacc, x, Wq, bq, Wk, bk, Wv, bv, Wo, bo, gate_w, sgate_w, w13, w2, sgu, sdn, stages=3):
    f32 = np.float32
    x, Wq, bq, Wk, bk, Wv, bv, Wo, bo, gate_w, sgate_w, w13, w2, sgu, sdn = (
        np.asarray(a) for a in (x, Wq, bq, Wk, bk, Wv, bv, Wo, bo, gate_w, sgate_w, w13, w2, sgu, sdn))

    def lhs(rows):
        full = np.zeros((MT * P, D), f32)
        full[:len(rows)] = rows
        return full.reshape(MT, P, KC, P).transpose(0, 3, 2, 1).reshape(MT, P, D)

    gate_rows = np.concatenate([w13[:, :FE].reshape(FEXP, D), sgu[:FS]])
    up_rows = np.concatenate([w13[:, FE:].reshape(FEXP, D), sgu[FS:]])
    down = np.zeros((MT * P, D), f32)
    down[:FEXP + FS] = np.concatenate([w2.transpose(0, 2, 1).reshape(FEXP, D), sdn.T])
    w = np.concatenate([lhs(gate_rows), lhs(up_rows), down.reshape(MT, P, D)], axis=2)
    gates = np.concatenate([gate_w, sgate_w]).T.reshape(KC, P, NG).transpose(1, 0, 2)
    order = np.arange(QW).reshape(GHI, GLO, GQ, HD).transpose(0, 2, 1, 3).reshape(-1)
    qkvo = np.concatenate([Wq[:, order], Wk, Wv, Wo], axis=1).reshape(KC, P, QKV + D).transpose(1, 0, 2)
    biases = np.broadcast_to(np.concatenate([bq[order], bk, bv, bo]), (P, QKV + D))
    inv = (f32(1.0) / np.power(f32(10000.0), np.arange(0, HD, 2, dtype=f32) / f32(HD))).astype(f32)
    ang = np.repeat(np.outer(np.arange(T, dtype=f32), inv).astype(f32), 2, axis=1)
    sign = np.tile(np.array([-1.0, 1.0], f32), HD // 2)
    rope = np.stack([np.cos(ang), np.sin(ang) * sign]).astype(f32).reshape(2, TT, P, HD).transpose(2, 0, 1, 3)
    ident = np.eye(P, dtype=f32)
    after = np.triu(np.full((P, P), NEG, f32), 1)
    mask = np.stack([after, after.T], axis=1)
    arrays = {"x_dram": x.reshape(T, D), "w_dram": w, "gate_dram": gates, "qkvo_dram": qkvo, "bias_dram": biases,
              "rope_dram": rope, "ident_dram": ident, "mask_dram": mask}
    arrays = {k: np.ascontiguousarray(a) for k, a in arrays.items()}
    nc = bacc.Bacc("TRN2", target_bir_lowering=False, num_devices=1)
    aps = [nc.dram_tensor(k, a.shape, F32, kind="ExternalInput").ap() for k, a in arrays.items()]
    out = nc.dram_tensor("out_dram", (T, D), F32, kind="ExternalOutput").ap()
    build(nc, *aps, out, stages=stages)
    return nc, arrays, x.shape
```

```python
import concourse.bass as bass
from concourse import mybir
from contextlib import ExitStack

F32, F16, BF16 = mybir.dt.float32, mybir.dt.float16, mybir.dt.bfloat16
ALU, ACT, AX = mybir.AluOpType, mybir.ActivationFunctionType, mybir.AxisListType

P = 128
T, D = 1024, 256
TT = T // P
KC = D // P
NE, FE, FS = 16, 176, 704
TOPK = 4
FEXP = NE * FE
MX = FEXP // P
MT = -(-(FEXP + FS) // P)
WC = 3 * D
NG = NE + 1
NC = 2
CH = T // NC
TPC = TT // NC
NH, NKV, HD = 32, 8, 8
GQ = NH // NKV
QW, KW = NH * HD, NKV * HD
QKV = QW + 2 * KW
ROW = 32
GLO = P // ROW
GHI = NKV // GLO
EPS = 1e-5
WS = 64.0
NEG = -1.0e30
SCALE = HD ** -0.5
RING = 3
LEAD = (0.0, 0.0, 0.0, 0.0)
ORDER = (2, 3, 7, 6, 5, 4, 1, 0)
RINGED = ("pj", "kx", "q1", "m", "q2", "f1", "f2b", "f3")


def coefficient_spans():
    spans = []
    for m in range(MT):
        f0 = m * P
        if m < MX:
            e = f0 // FE
            cut = min(P, (e + 1) * FE - f0)
            nxt = e + 1
        else:
            e, cut, nxt = NE, P, NE
        if cut == P:
            cut, nxt = P // 2, e
        spans.append([(m, 0, cut, e), (m, cut, P - cut, nxt)])
    return spans


def attention_schedule():
    PE, DVE, ACTE, POOL = range(4)
    streams = [[], [], [], []]
    for t in range(-2, TT):
        streams[1] += [("sp", t)] * (t >= 0) + [("pj", t + 2)] * (t + 2 < TT) + [("kx", t)] * (t >= 0)
    k = 0
    for i, t in enumerate(ORDER):
        streams[0].append(("q1", i))
        for h in range(NH):
            for kc in range(t // 4 + 1):
                streams[0].append(("m", k, i, h, kc))
                k += 1
        streams[0] += [("mx", i), ("q2", i)]
    n, last = 0, None
    for i, t in enumerate(ORDER):
        for g in range(GHI):
            for kt in range(t + 1):
                streams[3] += [("st", n, pair, 2 * i + g, g, kt, i) for pair in range(2)]
                if last:
                    streams[3].append(("pv",) + last)
                    if last[3] == ORDER[last[4]]:
                        streams[3].append(("o", last[1]))
                last = (n, 2 * i + g, g, kt, i)
                n += 1
        streams[2] += [("f1", 2 * i), ("f1", 2 * i + 1), ("f2a", i), ("f2b", i), ("f3", i)]
    streams[3] += [("pv",) + last, ("o", last[1])]

    def work(e):
        kind, t = e[0], e[1]
        if kind == "pj":
            return [(PE, 1.0), (DVE, 1.2), (POOL, 1.8)], [("sp", t - 2)]
        if kind == "sp":
            return [(ACTE, 0.9), (DVE, 0.7)], [("pj", t)]
        if kind == "kx":
            return [(PE, 0.15), (ACTE, 1.1)], [("sp", t)]
        if kind == "q1":
            return [(PE, 0.5), (ACTE, 1.0)], [("kx", ORDER[t])]
        if kind == "m":
            cols = min(4, ORDER[e[2]] + 1 - 4 * e[4]) * P
            return [(PE, 0.06 + cols / 2400), (DVE, 0.07 + cols / 960)], [("q1", e[2])]
        if kind == "mx":
            return [(DVE, 0.6)], []
        if kind == "q2":
            return [(PE, 0.5), (ACTE, 1.0)], [("mx", t), ("last_st", t - 2)]
        if kind == "st":
            diag = e[5] == ORDER[e[6]]
            return [(PE, 0.9 if diag else 0.45), (ACTE, 0.95)], [("q2", e[6]), ("st", e[1] - 1, e[2])]
        if kind == "pv":
            return [(PE, 1.4)], [("st", t, 1), ("o", e[2] - 1)] + [("pj", e[4])] 
        if kind == "o":
            return [(ACTE, 0.55)], [("last_pv", t), ("f1", t - 2)]
        if kind == "f1":
            return [(PE, 0.5), (DVE, 0.9)], [("o", t), ("f2a", t // 2 - 1)]
        if kind == "f2a":
            return [(ACTE, 0.3), (DVE, 0.4)], [("f1", 2 * t + 1)]
        if kind == "f2b":
            return [(PE, 0.25), (ACTE, 0.55)], [("f2a", t)]
        return [(PE, 0.7), (DVE, 0.4)], [("f2b", t)]

    free, done, ring, events, at = [0.0] * 4, {}, [0.0] * RING, [], [0] * 4

    def start(e):
        ops, after = work(e)
        begin = free[ops[0][0]]
        for a in after:
            if min(x for x in a[1:2]) < 0:
                continue
            if a not in done:
                return None
            begin = max(begin, done[a])
        if e[0] in RINGED:
            begin = max(begin, ring[0])
        return begin

    while any(at[i] < len(streams[i]) for i in range(4)):
        ready = [(b, i) for i in range(4) if at[i] < len(streams[i])
                 for b in [start(streams[i][at[i]])] if b is not None]
        _, i, begin = min((b - LEAD[i], i, b) for b, i in ready)
        e = streams[i][at[i]]
        at[i] += 1
        now = begin
        for engine, cost in work(e)[0]:
            now = max(now, free[engine]) + cost
            free[engine] = now
            now += 0.15
        done[e if e[0] != "st" else e[:3]] = now
        if e[0] == "pv" and e[4] == ORDER[e[5]]:
            done[("last_pv", e[2])] = now
        if e[0] == "st" and e[2:3] + e[4:6] == (1, GHI - 1, ORDER[e[6]]):
            done[("last_st", e[6])] = now
        if e[0] in RINGED:
            ring = ring[1:] + [now]
        events.append(e)
    return events


def build(nc, x_in, w_in, gate_in, qkvo_in, bias_in, rope_in, ident_in, mask_in, out, stages=3):
    ctx = ExitStack()
    with ctx:
        def sb(name, shape, dt):
            return ctx.enter_context(nc.sbuf_tensor(name, shape, dt))

        def sem(name):
            return ctx.enter_context(nc.semaphore(name))

        psum = ctx.enter_context(nc.psum_tensor("psum", [P, 8 * 512], F32))
        bank = [psum[:, 512 * i:512 * (i + 1)] for i in range(8)]
        coef_dram = [nc.dram_tensor(f"coef_dram{f}", (NG, T), F32).ap() for f in range(2)]

        x_res = sb("x_res", [P, TT, D], F32)
        xT = sb("xT", [P, 2, KC, T], F16)
        W_hi = sb("W_hi", [P, MT, WC], F16)
        W_lo = sb("W_lo", [P, MT, WC], F16)
        gate_f = sb("gate_f", [P, KC, NG], F32)
        gate_h = sb("gate_h", [P, 2, KC, NG], F16)
        qkvo_h = sb("qkvo_h", [P, 2, KC, QKV + D], F16)
        bias = sb("bias", [P, QKV + D], F32)
        rope = sb("rope", [P, 2, TT, HD], F32)
        ident = sb("ident", [P, P], F32)
        ident16 = sb("ident16", [P, P], F16)
        identb = sb("identb", [P, P], BF16)
        maskf = sb("maskf", [P, 2, P], F32)
        maskb = sb("maskb", [P, 2, P], BF16)
        w_stage = sb("w_stage", [P, 2, WC], F32)

        R1 = sb("R1", [P, 4096], F32)
        R2 = sb("R2", [P, 4096], F32)
        xn = R1[:, 0:2048].rearrange("p (t d) -> p t d", t=TT)
        x_hl = R1[:, 2048:4096].bitcast(F16).rearrange("p (a t d) -> p a t d", a=2, t=TT)
        v = R1[:, 0:2048].rearrange("p (s c n) -> p s c n", s=2, c=NC)
        hc = R1[:, 2048:3072].rearrange("p (c n) -> p c n", c=NC)
        sg = R1[:, 3072:4096].rearrange("p (c n) -> p c n", c=NC)
        hT = R2[:, 0:2048].bitcast(F16).rearrange("p (a s n) -> p a s n", a=2, s=2)
        C = R2[:, 2048:4096].rearrange("p (s n) -> p s n", s=2)
        qaug = R2[:, :].bitcast(F16).rearrange("p (t h r) -> p t h r", t=TT, r=ROW)
        prob = R1[:, :].rearrange("p (s g n) -> p s g n", s=2, g=GLO)
        kT = sb("kT", [P, NKV, T], F16)
        qkvo_f = kT[:, :, :].rearrange("p g n -> p (g n)").bitcast(F32)[:, 0:KC * (QKV + D)]\
            .rearrange("p (k n) -> p k n", k=KC)
        kaug = sb("kaug", [P, TT, NKV, ROW], F16)
        vals = sb("vals", [P, TT, NKV, 32], F32)
        qkv = sb("qkv", [P, 2, QKV], F32)
        rot_a = sb("rot_a", [P, 2, QW + KW], F32)
        rot_b = sb("rot_b", [P, 2, QW + KW], F32)
        qT1 = sb("qT1", [P, 2, GHI * GQ, P], F16)
        qT2 = sb("qT2", [P, 2, GHI * GQ, P], F16)
        m_part = sb("m_part", [P, NH, 2], F32)
        m_row = sb("m_row", [P, NH], F32)
        oT = sb("oT", [P, 2, 512], F32)
        o_rs = sb("o_rs", [P, 2, GQ, GLO], F32)
        o_tok = sb("o_tok", [P, D], F32)
        o_hl = sb("o_hl", [P, 2, D], F16)
        oTT = sb("oTT", [P, 2, KC, P], F16)
        st = sb("st", [P, TT, 6], F32)
        mv = sb("mv", [P, TT, 2], F32)
        sd = sb("sd", [P, TT], F32)
        rs = sb("rs", [P, TT], F32)
        lg = sb("lg", [P, TT, NG], F32)
        mx = sb("mx", [P, TT], F32)
        ex = sb("ex", [P, TT, NG], F32)
        den = sb("den", [P, TT, 2], F32)
        rden = sb("rden", [P, TT, 2], F32)
        pr = sb("pr", [P, TT, NE + TOPK], F32)
        top = sb("top", [P, TT, 8], F32)
        rest = sb("rest", [P, TT, NE + TOPK], F32)
        cf = sb("cf", [P, TT, NG], F32)
        cT = oT[0:NG, :, :].rearrange("p a n -> p (a n)")

        s_x = [sem(f"s_x{t}") for t in range(TT)]
        s_const = sem("s_const")
        s_late = sem("s_late")
        s_qkvo = sem("s_qkvo")
        s_w = [sem(f"s_w{i}") for i in range(2)]
        s_dve = sem("s_dve")
        s_pool = sem("s_pool")
        s_whi = sem("s_whi")
        s_wlo = sem("s_wlo")
        s_ghi = sem("s_ghi")
        s_glo = sem("s_glo")
        s_var = sem("s_var")
        s_sd = sem("s_sd")
        s_xn = sem("s_xn")
        s_xh = sem("s_xh")
        s_xl = sem("s_xl")
        s_xps = sem("s_xps")
        s_xT = sem("s_xT")
        s_lg = sem("s_lg")
        s_d = sem("s_d")
        s_ex = sem("s_ex")
        s_cf = sem("s_cf")
        s_cps = sem("s_cps")
        s_cT = sem("s_cT")
        s_cdram = sem("s_cdram")
        s_C = [sem(f"s_C{i}") for i in range(2)]
        s_gu = [sem(f"s_gu{c}") for c in range(NC)]
        s_sg = [sem(f"s_sg{c}") for c in range(NC)]
        s_v = [sem(f"s_v{c}") for c in range(NC)]
        s_hc = [sem(f"s_hc{c}") for c in range(NC)]
        s_hhi = [sem(f"s_hhi{c}") for c in range(NC)]
        s_hlo = [sem(f"s_hlo{c}") for c in range(NC)]
        s_y = [sem(f"s_y{c}") for c in range(NC)]
        s_res = sem("s_res")
        s_ident = sem("s_ident")
        s_out = sem("s_out")
        s_qkvo_h = sem("s_qkvo_h")
        s_qkvo_l = sem("s_qkvo_l")
        s_ready = sem("s_ready")
        s_xb = sem("s_xb")
        s_vals = sem("s_vals")
        s_swap = sem("s_swap")
        s_rot = sem("s_rot")
        s_qkhi = sem("s_qkhi")
        s_qklo = sem("s_qklo")
        s_fill = [sem(f"s_fill{i}") for i in range(RING)]
        s_free = [sem(f"s_free{i}") for i in range(RING)]
        s_m = sem("s_m")
        s_st = sem("s_st")
        s_exp = sem("s_exp")
        s_pv = sem("s_pv")
        s_oT = sem("s_oT")
        s_ohi = sem("s_ohi")
        s_olo = sem("s_olo")
        N_CONST, N_LATE = 2 * 16, 3 * 16
        events = attention_schedule()
        turn = {e: n for n, e in enumerate(e for e in events if e[0] in RINGED)}
        last_m = {e[2]: e for e in events if e[0] == "m"}
        ring_bank = [bank[4], bank[5], bank[7]]
        unit_end = {e[2]: e[1] + 1 for e in events if e[0] == "pv"}

        def filled(eng, e):
            eng.wait_ge(s_fill[turn[e] % RING], turn[e] // RING + 1)
            return ring_bank[turn[e] % RING]

        def taken(eng, e):
            eng.wait_ge(s_free[turn[e] % RING], turn[e] // RING + 1)

        def free_of(e):
            return s_free[turn[e] % RING]

        block = ctx.enter_context(nc.Block())

        @block.sync
        def _(sp):
            xv = x_in.rearrange("(t p) d -> t p d", p=P)
            for t in range(TT):
                sp.dma_start(x_res[:, t, :], xv[t]).then_inc(s_x[t], 16)
                if t == TPC - 1:
                    sp.dma_start(ident[:], ident_in).then_inc(s_const, 16)
                    sp.dma_start(gate_f[:], gate_in).then_inc(s_const, 16)
            sp.dma_start(maskf[:], mask_in).then_inc(s_late, 16)
            sp.dma_start(bias[:], bias_in).then_inc(s_late, 16)
            sp.dma_start(rope[:], rope_in).then_inc(s_late, 16)
            sp.dma_start(qkvo_f, qkvo_in).then_inc(s_qkvo, 16)

            def coefficients(f):
                sp.wait_ge(s_cT, 2 * (f + 1))
                sp.dma_start(coef_dram[f], cT).then_inc(s_cdram, 16)
                sp.wait_ge(s_cdram, 16 * (f + 1))
                for m, pair in enumerate(coefficient_spans()):
                    M = f * MT + m
                    if M >= 2:
                        sp.wait_ge(s_hc[0], M - 1)
                        sp.wait_ge(s_hc[1], M - 1)
                    for _, p0, n, e in pair:
                        sp.dma_start(C[p0:p0 + n, m % 2, :],
                                     coef_dram[f][e:e + 1, :].to_broadcast([n, T])).then_inc(s_C[m % 2], 16)

            coefficients(0)
            if stages == 3:
                coefficients(1)
            ov = out.rearrange("(t p) d -> p t d", p=P)
            for b in range(4):
                sp.wait_ge(s_res, {1: b + 1, 2: 4, 3: 4 + b + 1}[stages])
                if stages == 2:
                    taken(sp, ('f3', ORDER.index(2 * b)))
                    taken(sp, ('f3', ORDER.index(2 * b + 1)))
                sp.dma_start(ov[:, 2 * b:2 * b + 2, :], x_res[:, 2 * b:2 * b + 2, :]).then_inc(s_out, 16)
            sp.wait_ge(s_out, 64)

        @block.gpsimd
        def _(pool):
            def weighted(f, m, j, c):
                M = f * MT + m
                pool.wait_ge(s_v[c], M + 1)
                pool.wait_ge(s_C[j], 32 * (M // 2 + 1) if isinstance(M, int) else 16 * (M - j) + 32)
                if not isinstance(M, int) or M >= 1:
                    pool.wait_ge(s_hlo[c], M)
                nc.gpsimd.tensor_tensor(hc[:, c, :], v[:, j, c, :], C[:, j, c * CH:(c + 1) * CH],
                                        ALU.mult).then_inc(s_hc[c], 1)

            def constants():
                pool.wait_ge(s_qkvo_l, 1)
                nc.gpsimd.memset(kT[:, :, :].rearrange("p g n -> p (g n)").bitcast(F32), 0.0)
                nc.gpsimd.memset(kaug[:], 0.0)
                nc.gpsimd.memset(vals[:], 0.0).then_inc(s_pool, 1)
                pool.wait_ge(s_pool, 1)
                nc.gpsimd.memset(kaug[:, :, :, 24:26], 1.0)
                nc.gpsimd.memset(vals[:, :, :, HD:HD + 1], 1.0).then_inc(s_ready, 1)

            def ffn(f, between=None):
                def step(s, j):
                    for c in range(NC):
                        weighted(f, s - 1, 1 - j, c)
                step(1, 1)
                step(2, 0)
                if between:
                    between()
                step(3, 1)
                with pool.Fori(2, MT // 2 - 1) as i:
                    step(2 * i, 0)
                    step(2 * i + 1, 1)
                step(MT - 2, 0)
                step(MT - 1, 1)
                for c in range(NC):
                    weighted(f, MT - 1, 1, c)

            ffn(0, constants)
            if stages == 1:
                return
            for c in range(NC):
                pool.wait_ge(s_y[c], MT)
            nc.gpsimd.memset(qaug[:, :, :, 24:32], 0.0).then_inc(s_ready, 1)
            for t in range(TT):
                taken(pool, ("pj", t))
                if t >= 2:
                    pool.wait_ge(s_qklo, t - 1)
                cos = rope[:, 0, t, :].unsqueeze(1).to_broadcast([P, NH + NKV, HD])
                ra = rot_a[:, t % 2, :]
                nc.gpsimd.tensor_tensor(ra.rearrange("p (h d) -> p h d", d=HD),
                                        qkv[:, t % 2, 0:QW + KW].rearrange("p (h d) -> p h d", d=HD),
                                        cos, ALU.mult).then_inc(s_pool, 1)
                pool.wait_ge(s_pool, 2 + t)
                pool.wait_ge(s_swap, t + 1)
                nc.gpsimd.tensor_tensor(ra, ra, rot_b[:, t % 2], ALU.add).then_inc(s_rot, 1)
            pool.wait_ge(s_xn, 2 * TT)
            for t in range(TT):
                nc.gpsimd.tensor_tensor(x_res[:, t, :], x_res[:, t, :], bias[:, QKV:QKV + D],
                                        ALU.add).then_inc(s_xb, 1)
            if stages == 3:
                ffn(1)

        @block.scalar
        def _(act):
            def load_weights(m, j):
                if not isinstance(m, int) or m >= 2:
                    act.wait_ge(s_wlo, m - 1)
                src = w_in[m] if isinstance(m, int) else w_in[bass.ds(m, 1), :, :].rearrange("o p n -> p (o n)")
                act.dma_start(w_stage[:, j, :], src).then_inc(s_w[j], 16)

            def weights_high(m, j):
                act.wait_ge(s_w[j], 16 * (m // 2 + 1) if isinstance(m, int) else 8 * (m - j) + 16)
                nc.scalar.activation(W_hi[:, m, :], w_stage[:, j, :], ACT.Copy, scale=WS).then_inc(s_whi, 1)

            def layer_norm(r):
                def deviation(h):
                    act.wait_ge(s_var, 2 * r + h + 1)
                    half = slice(h * TPC, (h + 1) * TPC)
                    nc.scalar.activation(sd[:, half], mv[:, half, 1], ACT.Sqrt).then_inc(s_sd, 1)

                def high_part(t):
                    act.wait_ge(s_xn, r * TT + t + 1)
                    nc.scalar.activation(x_hl[:, 0, t, :], xn[:, t, :], ACT.Copy).then_inc(s_xh, 1)

                def evacuate(t):
                    act.wait_ge(s_xps, r * TT + t + 1)
                    ps = bank[t % 4][:, 0:256].bitcast(F16).rearrange("p (a k n) -> p a k n", a=2, k=KC)
                    nc.scalar.activation(xT[:, :, :, t * P:(t + 1) * P], ps, ACT.Copy).then_inc(s_xT, 1)

                deviation(0)
                high_part(0)
                high_part(1)
                deviation(1)
                for t in range(TT):
                    evacuate(t)
                    if t + 2 < TT:
                        high_part(t + 2)

            def silu(f, m, c):
                M = f * MT + m
                act.wait_ge(s_gu[c], M + 1)
                if not isinstance(M, int) or M >= 1:
                    act.wait_ge(s_v[c], M)
                nc.scalar.activation(sg[:, c, :], bank[c][:, :], ACT.Silu, scale=1.0 / WS).then_inc(s_sg[c], 1)

            def high(f, m, j, c):
                M = f * MT + m
                act.wait_ge(s_hc[c], M + 1)
                if not isinstance(M, int) or M >= 2:
                    act.wait_ge(s_y[c], M - 1)
                nc.scalar.activation(hT[:, 0, j, c * CH:(c + 1) * CH], hc[:, c, :], ACT.Copy).then_inc(s_hhi[c], 1)

            def ffn(f):
                act.wait_ge(s_d, f + 1)
                nc.scalar.activation(ex[:], lg[:], ACT.Exp).then_inc(s_ex, 1)

                def step(s, j):
                    if f == 0 and (not isinstance(s, int) or s + 2 < MT):
                        load_weights(s + 2, j)
                    if f == 0 and (not isinstance(s, int) or s + 1 < MT):
                        weights_high(s + 1, 1 - j)
                    for c in range(NC):
                        silu(f, s, c)
                        if not isinstance(s, int) or s >= 2:
                            high(f, s - 1, 1 - j, c)
                step(0, 0)
                for h in range(2):
                    act.wait_ge(s_cps, 2 * f + h + 1)
                    nc.scalar.activation(cT[:, h * 512:(h + 1) * 512], bank[7 - h][0:NG, :],
                                         ACT.Copy).then_inc(s_cT, 1)
                step(1, 1)
                for c in range(NC):
                    high(f, 0, 0, c)
                step(2, 0)
                step(3, 1)
                with act.Fori(2, MT // 2 - 1) as i:
                    step(2 * i, 0)
                    step(2 * i + 1, 1)
                step(MT - 2, 0)
                step(MT - 1, 1)
                for c in range(NC):
                    high(f, MT - 1, 1, c)

            load_weights(0, 0)
            load_weights(1, 1)
            act.wait_ge(s_const, N_CONST)
            nc.scalar.activation(gate_h[:, 0], gate_f[:], ACT.Copy, scale=WS).then_inc(s_ghi, 1)
            weights_high(0, 0)
            layer_norm(0)
            act.wait_ge(s_qkvo, 16)
            nc.scalar.activation(qkvo_h[:, 0], qkvo_f, ACT.Copy, scale=WS).then_inc(s_qkvo_h, 1)
            ffn(0)
            if stages == 1:
                return
            layer_norm(1)

            for e in events:
                kind, t = e[0], e[1]
                if kind == "sp":
                    act.wait_ge(s_rot, t + 1)
                    if t == 0:
                        act.wait_ge(s_ready, 2)
                    q = rot_a[:, t % 2, 0:QW].rearrange("p (h d) -> p h d", d=HD).unsqueeze(2)
                    k = rot_a[:, t % 2, QW:QW + KW].rearrange("p (h d) -> p h d", d=HD).unsqueeze(2)
                    nc.scalar.activation(qaug[:, t].rearrange("p h (a d) -> p h a d", d=HD)[:, :, 0:4:2, :],
                                         q.to_broadcast([P, NH, 2, HD]), ACT.Copy)
                    nc.scalar.activation(kaug[:, t].rearrange("p h (a d) -> p h a d", d=HD)[:, :, 0:2, :],
                                         k.to_broadcast([P, NKV, 2, HD]), ACT.Copy).then_inc(s_qkhi, 1)
                elif kind == "kx":
                    ps = filled(act, e)[:, 0:P].bitcast(F16).rearrange("p (a n) -> p a n", a=GHI)
                    for g in range(GLO):
                        rows = slice(ROW * g, ROW * (g + 1))
                        ins = nc.scalar.activation(kT[rows, g:NKV:GLO, t * P:(t + 1) * P], ps[rows], ACT.Copy)
                    ins.then_inc(free_of(e), 1)
                elif kind in ("q1", "q2"):
                    ps = filled(act, e)
                    dst = qT1 if kind == "q1" else qT2
                    nc.scalar.activation(dst[:, t % 2].rearrange("p a n -> p (a n)"), ps.bitcast(F16),
                                         ACT.Copy).then_inc(free_of(e), 1)
                elif kind == "st":
                    n, pair = e[1], e[2]
                    act.wait_ge(s_st, 2 * n + pair + 1)
                    if n >= 2:
                        act.wait_ge(s_pv, n - 1)
                    nc.scalar.activation(prob[:, n % 2, 2 * pair:2 * pair + 2, :].rearrange("p g n -> p (g n)"),
                                         psum[:, 1024 * pair:1024 * (pair + 1)], ACT.Exp,
                                         scale=SCALE).then_inc(s_exp, 1)
                elif kind == "o":
                    u = t
                    act.wait_ge(s_pv, unit_end[u])
                    if u >= 2:
                        taken(act, ("f1", u - 2))
                    nc.scalar.activation(oT[:, u % 2, :], bank[6], ACT.Copy).then_inc(s_oT, 1)
                elif kind == "f2a":
                    taken(act, ("f1", 2 * t))
                    taken(act, ("f1", 2 * t + 1))
                    nc.scalar.activation(o_hl[:, 0], o_tok[:], ACT.Copy).then_inc(s_ohi, 1)
                elif kind == "f2b":
                    ps = filled(act, e)
                    nc.scalar.activation(oTT[:, :, :, :].rearrange("p a k n -> p (a k n)"),
                                         ps[:, 0:256].bitcast(F16), ACT.Copy).then_inc(free_of(e), 1)
            if stages == 3:
                layer_norm(2)
                ffn(1)

        @block.vector
        def _(dve):
            chain = [0]

            def link(ins):
                chain[0] += 1
                ins.then_inc(s_dve, 1)
                dve.wait_ge(s_dve, chain[0])

            def layer_norm(r):
                def statistics(h):
                    tiles = range(h * TPC, (h + 1) * TPC)
                    for t in tiles:
                        if r == 0:
                            dve.wait_ge(s_x[t], 16)
                        elif r == 1:
                            dve.wait_ge(s_res, t // 2 + 1)
                        else:
                            taken(dve, ("f3", ORDER.index(t)))
                        ins = nc.vector.bn_stats(st[:, t, :], x_res[:, t, :])
                    link(ins)
                    for t in tiles:
                        ins = nc.vector.bn_aggr(mv[:, t, :], st[:, t, :])
                    link(ins)
                    var = mv[:, h * TPC:(h + 1) * TPC, 1]
                    nc.vector.tensor_scalar(var, var, EPS, None, ALU.add).then_inc(s_var, 1)

                def normalise(t):
                    if t % TPC == 0:
                        h = t // TPC
                        dve.wait_ge(s_sd, 2 * r + h + 1)
                        half = slice(h * TPC, (h + 1) * TPC)
                        link(nc.vector.reciprocal(rs[:, half], sd[:, half]))
                    nc.vector.tensor_scalar(xn[:, t, :], x_res[:, t, :], mv[:, t, 0:1], rs[:, t:t + 1],
                                            ALU.subtract, ALU.mult).then_inc(s_xn, 1)

                def low_part(t):
                    dve.wait_ge(s_xh, r * TT + t + 1)
                    nc.vector.tensor_tensor(x_hl[:, 1, t, :], xn[:, t, :], x_hl[:, 0, t, :],
                                            ALU.subtract).then_inc(s_xl, 1)

                statistics(0)
                if r == 0:
                    dve.wait_ge(s_const, N_CONST)
                    nc.vector.tensor_copy(ident16[:], ident[:]).then_inc(s_ident, 1)
                normalise(0)
                normalise(1)
                if r == 1:
                    residual(0, 1)
                statistics(1)
                for t in range(TT):
                    low_part(t)
                    if t + 2 < TT:
                        normalise(t + 2)

            def residual(f, c):
                dve.wait_ge(s_y[c], (f + 1) * MT)
                for b in (2 * c, 2 * c + 1):
                    xr = x_res[:, 2 * b:2 * b + 2, :]
                    nc.vector.scalar_tensor_tensor(out=xr, in0=bank[4 + b].rearrange("p (t d) -> p t d", t=2),
                                                   scalar=0.5 / WS, in1=xr, op0=ALU.mult,
                                                   op1=ALU.add).then_inc(s_res, 1)

            def router(f):
                dve.wait_ge(s_lg, f + 1)
                link(nc.vector.tensor_scalar(lg[:], bank[6][:, 0:TT * NG].rearrange("p (t e) -> p t e", t=TT),
                                             1.0 / WS, None, ALU.mult))
                link(nc.vector.tensor_reduce(mx[:], lg[:, :, 0:NE], axis=AX.X, op=ALU.max))
                nc.vector.tensor_tensor(lg[:, :, 0:NE], lg[:, :, 0:NE],
                                        mx[:, :].unsqueeze(2).to_broadcast([P, TT, NE]), ALU.subtract)
                nc.vector.tensor_scalar(lg[:, :, NE:NG], lg[:, :, NE:NG], -1.0, None, ALU.mult).then_inc(s_d, 1)
                dve.wait_ge(s_ex, f + 1)
                nc.vector.tensor_reduce(den[:, :, 0:1], ex[:, :, 0:NE], axis=AX.X, op=ALU.add)
                link(nc.vector.tensor_scalar(den[:, :, 1:2], ex[:, :, NE:NG], 1.0, None, ALU.add))
                link(nc.vector.reciprocal(rden[:], den[:]))
                nc.vector.tensor_tensor(pr[:, :, 0:NE], ex[:, :, 0:NE],
                                        rden[:, :, 0:1].to_broadcast([P, TT, NE]), ALU.mult)
                link(nc.vector.tensor_copy(cf[:, :, NE:NG], rden[:, :, 1:2]))
                for t in range(TT):
                    ins = nc.vector.max(top[:, t, :], pr[:, t, :])
                link(ins)
                link(nc.vector.memset(top[:, :, TOPK:8], -1.0))
                for t in range(TT):
                    ins = nc.vector.match_replace(out=rest[:, t, :], in_to_replace=top[:, t, :],
                                                  in_values=pr[:, t, :], imm_value=0.0)
                link(ins)
                nc.vector.tensor_tensor(cf[:, :, 0:NE], pr[:, :, 0:NE], rest[:, :, 0:NE],
                                        ALU.subtract).then_inc(s_cf, 1)

            def weights_low(m, j):
                dve.wait_ge(s_whi, m + 1)
                nc.vector.scalar_tensor_tensor(out=W_lo[:, m, :], in0=w_stage[:, j, :], scalar=WS,
                                               in1=W_hi[:, m, :], op0=ALU.mult,
                                               op1=ALU.subtract).then_inc(s_wlo, 1)

            def gated(f, m, j, c):
                M = f * MT + m
                dve.wait_ge(s_sg[c], M + 1)
                if not isinstance(M, int) or M >= 2:
                    dve.wait_ge(s_hc[c], M - 1)
                nc.vector.scalar_tensor_tensor(out=v[:, j, c, :], in0=bank[2 + c][:, :], scalar=1.0 / WS,
                                               in1=sg[:, c, :], op0=ALU.mult, op1=ALU.mult).then_inc(s_v[c], 1)

            def low(f, m, j, c):
                M = f * MT + m
                dve.wait_ge(s_hhi[c], M + 1)
                nc.vector.tensor_tensor(hT[:, 1, j, c * CH:(c + 1) * CH], hc[:, c, :],
                                        hT[:, 0, j, c * CH:(c + 1) * CH], ALU.subtract).then_inc(s_hlo[c], 1)

            def ffn(f):
                router(f)

                def step(s, j):
                    if f == 0 and (not isinstance(s, int) or s + 1 < MT):
                        weights_low(s + 1, 1 - j)
                    for c in range(NC):
                        gated(f, s, j, c)
                        if not isinstance(s, int) or s >= 2:
                            low(f, s - 1, 1 - j, c)
                step(0, 0)
                step(1, 1)
                if f == 0:
                    dve.wait_ge(s_late, N_LATE)
                    nc.vector.tensor_copy(identb[:], ident[:])
                    nc.vector.tensor_copy(maskb[:], maskf[:])
                    dve.wait_ge(s_qkvo_h, 1)
                    nc.vector.scalar_tensor_tensor(out=qkvo_h[:, 1], in0=qkvo_f, scalar=WS, in1=qkvo_h[:, 0],
                                                   op0=ALU.mult, op1=ALU.subtract).then_inc(s_qkvo_l, 1)
                for c in range(NC):
                    low(f, 0, 0, c)
                step(2, 0)
                step(3, 1)
                with dve.Fori(2, MT // 2 - 1) as i:
                    step(2 * i, 0)
                    step(2 * i + 1, 1)
                step(MT - 2, 0)
                step(MT - 1, 1)
                for c in range(NC):
                    low(f, MT - 1, 1, c)
                residual(f, 0)

            nc.vector.memset(pr[:, :, NE:NE + TOPK], -1.0)
            layer_norm(0)
            dve.wait_ge(s_ghi, 1)
            nc.vector.scalar_tensor_tensor(out=gate_h[:, 1], in0=gate_f[:], scalar=WS, in1=gate_h[:, 0],
                                           op0=ALU.mult, op1=ALU.subtract).then_inc(s_glo, 1)
            weights_low(0, 0)
            ffn(0)
            if stages == 1:
                return
            layer_norm(1)

            for e in events:
                kind, t = e[0], e[1]
                if kind == "pj":
                    ps = filled(dve, e)
                    if t >= 2:
                        dve.wait_ge(s_rot, t - 1)
                    nc.vector.scalar_tensor_tensor(out=qkv[:, t % 2, :], in0=ps[:, 0:QKV], scalar=1.0 / WS,
                                                   in1=bias[:, 0:QKV], op0=ALU.mult,
                                                   op1=ALU.add).then_inc(free_of(e), 1)
                    taken(dve, e)
                    if t == 0:
                        dve.wait_ge(s_ready, 1)
                    nc.vector.tensor_copy(vals[:, t, :, 0:HD],
                                          qkv[:, t % 2, QW + KW:QKV].rearrange("p (h d) -> p h d", d=HD)
                                          ).then_inc(s_vals, 1)
                    x = qkv[:, t % 2, 0:QW + KW].rearrange("p (h n e) -> p h n e", n=HD // 2, e=2)
                    sin = rope[:, 1, t, :].rearrange("p (n e) -> p n e", e=2).unsqueeze(1)\
                        .to_broadcast([P, NH + NKV, HD // 2, 2])
                    nc.vector.tensor_tensor(rot_b[:, t % 2].rearrange("p (h n e) -> p h n e", n=HD // 2, e=2),
                                            x[:, :, :, ::-1], sin, ALU.mult).then_inc(s_swap, 1)
                elif kind == "sp":
                    dve.wait_ge(s_qkhi, t + 1)
                    q = rot_a[:, t % 2, 0:QW].rearrange("p (h d) -> p h d", d=HD)
                    k = rot_a[:, t % 2, QW:QW + KW].rearrange("p (h d) -> p h d", d=HD)
                    nc.vector.tensor_tensor(qaug[:, t, :, HD:2 * HD], q, qaug[:, t, :, 0:HD], ALU.subtract)
                    nc.vector.tensor_tensor(kaug[:, t, :, 2 * HD:3 * HD], k, kaug[:, t, :, 0:HD],
                                            ALU.subtract).then_inc(s_qklo, 1)
                elif kind == "m":
                    _, k, i, h, kc = e
                    t = ORDER[i]
                    ps = filled(dve, e)
                    n = min(4, t + 1 - 4 * kc) * P
                    nc.vector.tensor_reduce(m_part[:, h, kc:kc + 1], ps[:, 0:n], axis=AX.X,
                                            op=ALU.max).then_inc(free_of(e), 1)
                elif kind == "mx":
                    i, t = t, ORDER[t]
                    taken(dve, last_m[i])
                    if t >= 4:
                        link(nc.vector.tensor_tensor(m_row[:], m_part[:, :, 0], m_part[:, :, 1], ALU.max))
                    else:
                        link(nc.vector.tensor_copy(m_row[:], m_part[:, :, 0]))
                    link(nc.vector.tensor_scalar(qaug[:, t, :, 24], m_row[:], -1.0, None, ALU.mult))
                    nc.vector.scalar_tensor_tensor(out=qaug[:, t, :, 25], in0=m_row[:], scalar=-1.0,
                                                   in1=qaug[:, t, :, 24], op0=ALU.mult,
                                                   op1=ALU.subtract).then_inc(s_m, 1)
                    dve.wait_ge(s_m, i + 1)
                elif kind == "f1":
                    u = t
                    ps = filled(dve, e).rearrange("p (j g r) -> p j g r", j=GQ, g=GLO)
                    if u >= 2:
                        taken(dve, ("f1", u - 2))
                    link(nc.vector.reciprocal(o_rs[:, u % 2], ps[:, :, :, HD]))
                    if u % 2 == 0 and u >= 2:
                        dve.wait_ge(s_olo, u // 2)
                    o = o_tok[:, (u % 2) * P:(u % 2 + 1) * P].rearrange("p (g j d) -> p j g d", g=GLO, j=GQ)
                    nc.vector.tensor_tensor(o, ps[:, :, :, 0:HD],
                                            o_rs[:, u % 2].unsqueeze(3).to_broadcast([P, GQ, GLO, HD]),
                                            ALU.mult).then_inc(free_of(e), 1)
                elif kind == "f2a":
                    dve.wait_ge(s_ohi, t + 1)
                    nc.vector.tensor_tensor(o_hl[:, 1], o_tok[:], o_hl[:, 0], ALU.subtract).then_inc(s_olo, 1)
                elif kind == "f3":
                    ps = filled(dve, e)
                    t = ORDER[t]
                    dve.wait_ge(s_xb, t + 1)
                    nc.vector.scalar_tensor_tensor(out=x_res[:, t, :], in0=ps[:, 0:D], scalar=1.0 / WS,
                                                   in1=x_res[:, t, :], op0=ALU.mult,
                                                   op1=ALU.add).then_inc(free_of(e), 1)
            if stages == 3:
                layer_norm(2)
                ffn(1)
                residual(1, 1)

        @block.tensor
        def _(pe):
            def split_product(o, stat, mov, k_parts, first=True, last=True, **kw):
                n = 0
                for k in range(k_parts):
                    for a, b in ((0, 0), (0, 1), (1, 0)):
                        ins = nc.tensor.matmul(o, stat(a, k), mov(b, k), start=first and n == 0,
                                               stop=last and n == 3 * k_parts - 1, **kw)
                        n += 1
                return ins

            def layer_norm(r):
                for t in range(TT):
                    pe.wait_ge(s_xl, r * TT + t + 1)
                    if t >= 4:
                        pe.wait_ge(s_xT, r * TT + t - 3)
                    ps = bank[t % 4][:, 0:256].bitcast(F16)
                    for a in range(2):
                        for k in range(KC):
                            q = a * KC + k
                            ins = nc.tensor.transpose(ps[:, q * P:(q + 1) * P],
                                                      x_hl[:, a, t, k * P:(k + 1) * P], ident16[:])
                    ins.then_inc(s_xps, 1)

            def gate_up(f, m, c):
                M = f * MT + m
                if f == 0:
                    pe.wait_ge(s_wlo, m + 1)
                if not isinstance(M, int) or M >= 1:
                    pe.wait_ge(s_v[c], M)
                parts = (W_hi, W_lo)
                for u in range(2):
                    ins = split_product(
                        bank[2 * u + c][:, :],
                        lambda a, k: parts[a][:, m, (2 * u + k) * P:(2 * u + k + 1) * P],
                        lambda b, k: xT[:, b, k, c * CH:(c + 1) * CH], KC)
                ins.then_inc(s_gu[c], 1)

            def down(f, m, j, c, first=False, last=False):
                M = f * MT + m
                pe.wait_ge(s_hlo[c], M + 1)
                parts = (W_hi, W_lo)
                for t in range(c * TPC, (c + 1) * TPC):
                    o = bank[4 + t // 2][:, (t % 2) * D:(t % 2 + 1) * D]
                    ins = split_product(o, lambda a, k: hT[:, a, j, t * P:(t + 1) * P],
                                        lambda b, k: parts[b][:, m, 2 * D:3 * D], 1,
                                        first=first and t % 2 == 0, last=last, skip_group_check=True)
                ins.then_inc(s_y[c], 1)

            def ffn(f):
                for t in range(TT):
                    pe.wait_ge(s_xT, f * 2 * TT + t + 1)
                    if f == 0 and t == 0:
                        pe.wait_ge(s_glo, 1)
                    ins = split_product(bank[6][:, t * NG:(t + 1) * NG],
                                        lambda a, k: xT[:, a, k, t * P:(t + 1) * P],
                                        lambda b, k: gate_h[:, b, k, :], KC)
                ins.then_inc(s_lg, 1)

                def step(s, j, **kw):
                    for c in range(NC):
                        gate_up(f, s, c)
                        if not isinstance(s, int) or s >= 2:
                            down(f, s - 2, j, c, **kw)
                step(0, 0)
                pe.wait_ge(s_cf, f + 1)
                for t in range(TT):
                    ins = nc.tensor.transpose(bank[7 - t // 4][0:NG, (t % 4) * P:(t % 4 + 1) * P],
                                              cf[:, t, :], ident[:])
                    if t % 4 == 3:
                        ins.then_inc(s_cps, 1)
                step(1, 1)
                for c in range(NC):
                    gate_up(f, 2, c)
                    if c == 0:
                        pe.wait_ge(s_cT, 2 * (f + 1))
                    down(f, 0, 0, c, first=True)
                step(3, 1)
                with pe.Fori(2, MT // 2 - 1) as i:
                    step(2 * i, 0)
                    step(2 * i + 1, 1)
                step(MT - 2, 0)
                step(MT - 1, 1)
                for c in range(NC):
                    down(f, MT - 2, 0, c)
                    down(f, MT - 1, 1, c, last=True)

            pe.wait_ge(s_ident, 1)
            layer_norm(0)
            ffn(0)
            if stages == 1:
                return
            layer_norm(1)

            for e in events:
                kind, t = e[0], e[1]
                if kind in RINGED:
                    k = turn[e]
                    out_bank, full = ring_bank[k % RING], s_fill[k % RING]
                    if k >= RING:
                        pe.wait_ge(s_free[k % RING], k // RING)
                if kind == "pj":
                    pe.wait_ge(s_xT, TT + t + 1)
                    split_product(out_bank[:, 0:QKV], lambda a, k: xT[:, a, k, t * P:(t + 1) * P],
                                  lambda b, k: qkvo_h[:, b, k, 0:QKV], KC).then_inc(full, 1)
                elif kind == "kx":
                    pe.wait_ge(s_qklo, t + 1)
                    ps = out_bank[:, 0:P].bitcast(F16)
                    for a in range(GHI):
                        ins = nc.tensor.transpose(ps[:, a * P:(a + 1) * P],
                                                  kaug[:, t, GLO * a:GLO * (a + 1), :].rearrange("p h r -> p (h r)"),
                                                  ident16[:])
                    ins.then_inc(full, 1)
                elif kind in ("q1", "q2"):
                    i, t = t, ORDER[t]
                    if kind == "q2":
                        pe.wait_ge(s_m, i + 1)
                    else:
                        taken(pe, ("kx", t))
                    ps = out_bank.bitcast(F16)
                    for q in range(GHI * GQ):
                        ins = nc.tensor.transpose(ps[:, q * P:(q + 1) * P],
                                                  qaug[:, t, GLO * q:GLO * (q + 1), :].rearrange("p h r -> p (h r)"),
                                                  ident16[:])
                    ins.then_inc(full, 1)
                elif kind == "m":
                    _, k, i, h, kc = e
                    t = ORDER[i]
                    if (h, kc) == (0, 0):
                        taken(pe, ("q1", i))
                    g = h // (GQ * GLO) * GLO + h % GLO
                    n = min(4, t + 1 - 4 * kc) * P
                    diag = kc == t // 4
                    if diag:
                        nc.tensor.matmul(out_bank[:, n - P:n], identb[:], maskb[:, 0, :],
                                         start=True, stop=False, skip_group_check=True)
                    nc.tensor.matmul(out_bank[:, 0:n], qT1[:, i % 2, h // GLO, :],
                                     kT[:, g, kc * 512:kc * 512 + n], start=not diag, stop=True,
                                     skip_group_check=diag).then_inc(full, 1)
                elif kind == "st":
                    _, n, pair, u, gh, kt, i = e
                    t = ORDER[i]
                    if n >= 1:
                        pe.wait_ge(s_exp, 2 * (n - 1) + pair + 1)
                    if kt == 0 and pair == 0:
                        taken(pe, ("q2", i))
                    for gl in (2 * pair, 2 * pair + 1):
                        ins = nc.tensor.matmul(bank[gl], kT[:, gh * GLO + gl, kt * P:(kt + 1) * P],
                                               qT2[:, i % 2, gh * GQ:(gh + 1) * GQ, :], start=True, stop=kt != t)
                        if kt == t:
                            ins = nc.tensor.matmul(bank[gl].rearrange("p (j n) -> p j n", j=GQ), identb[:],
                                                   maskb[:, 1, :].unsqueeze(1).to_broadcast([P, GQ, P]),
                                                   start=False, stop=True)
                    ins.then_inc(s_st, 1)
                elif kind == "pv":
                    _, n, u, gh, kt, i = e
                    t = ORDER[i]
                    pe.wait_ge(s_exp, 2 * n + 2)
                    if kt == 0:
                        pe.wait_ge(s_vals, t + 1)
                    if kt == 0 and u >= 1:
                        pe.wait_ge(s_oT, u)
                    for gl in range(GLO):
                        ins = nc.tensor.matmul(bank[6][32 * gl:32 * (gl + 1), :], vals[:, kt, gh * GLO + gl, :],
                                               prob[:, n % 2, gl, :], start=kt == 0, stop=kt == t)
                    ins.then_inc(s_pv, 1)
                elif kind == "f1":
                    u = t
                    pe.wait_ge(s_oT, u + 1)
                    for j in range(GQ):
                        ins = nc.tensor.transpose(out_bank[:, j * P:(j + 1) * P], oT[:, u % 2, j * P:(j + 1) * P],
                                                  ident[:])
                    ins.then_inc(full, 1)
                elif kind == "f2b":
                    pe.wait_ge(s_olo, t + 1)
                    ps = out_bank[:, 0:256].bitcast(F16)
                    for a in range(2):
                        for k in range(KC):
                            q = a * KC + k
                            ins = nc.tensor.transpose(ps[:, q * P:(q + 1) * P], o_hl[:, a, k * P:(k + 1) * P],
                                                      ident16[:])
                    ins.then_inc(full, 1)
                elif kind == "f3":
                    taken(pe, ("f2b", t))
                    split_product(out_bank[:, 0:D], lambda a, k: oTT[:, a, k, :],
                                  lambda b, k: qkvo_h[:, b, k, QKV:QKV + D], KC).then_inc(full, 1)
            if stages == 3:
                layer_norm(2)
                ffn(1)


def kernel(L0_attn_x, L0_attn_Wq, L0_attn_bq, L0_attn_Wk, L0_attn_bk, L0_attn_Wv, L0_attn_bv, L0_attn_Wo,
           L0_attn_bo, L0_ffn_gate_w, L0_ffn_sgate_w, L0_ffn_w13, L0_ffn_w2, L0_ffn_shared_gate_up_w,
           L0_ffn_shared_down_w, stages=3):
    import numpy as np
    import concourse.bacc as bacc
    from concourse.bass_utils import run_bass_kernel_spmd

    nc, arrays, shape = program_and_arrays(np, bacc, L0_attn_x, L0_attn_Wq, L0_attn_bq, L0_attn_Wk, L0_attn_bk,
                                           L0_attn_Wv, L0_attn_bv, L0_attn_Wo, L0_attn_bo, L0_ffn_gate_w,
                                           L0_ffn_sgate_w, L0_ffn_w13, L0_ffn_w2, L0_ffn_shared_gate_up_w,
                                           L0_ffn_shared_down_w, stages)
    r = run_bass_kernel_spmd(nc, [arrays], core_ids=[0])
    return r.results[0]["out_dram"].reshape(shape)


def program_and_arrays(np, bacc, x, Wq, bq, Wk, bk, Wv, bv, Wo, bo, gate_w, sgate_w, w13, w2, sgu, sdn, stages=3):
    f32 = np.float32
    x, Wq, bq, Wk, bk, Wv, bv, Wo, bo, gate_w, sgate_w, w13, w2, sgu, sdn = (
        np.asarray(a) for a in (x, Wq, bq, Wk, bk, Wv, bv, Wo, bo, gate_w, sgate_w, w13, w2, sgu, sdn))

    def lhs(rows):
        full = np.zeros((MT * P, D), f32)
        full[:len(rows)] = rows
        return full.reshape(MT, P, KC, P).transpose(0, 3, 2, 1).reshape(MT, P, D)

    gate_rows = np.concatenate([w13[:, :FE].reshape(FEXP, D), sgu[:FS]])
    up_rows = np.concatenate([w13[:, FE:].reshape(FEXP, D), sgu[FS:]])
    down = np.zeros((MT * P, D), f32)
    down[:FEXP + FS] = np.concatenate([w2.transpose(0, 2, 1).reshape(FEXP, D), sdn.T])
    w = np.concatenate([lhs(gate_rows), lhs(up_rows), down.reshape(MT, P, D)], axis=2)
    gates = np.concatenate([gate_w, sgate_w]).T.reshape(KC, P, NG).transpose(1, 0, 2)
    order = np.arange(QW).reshape(GHI, GLO, GQ, HD).transpose(0, 2, 1, 3).reshape(-1)
    qkvo = np.concatenate([Wq[:, order], Wk, Wv, Wo], axis=1).reshape(KC, P, QKV + D).transpose(1, 0, 2)
    biases = np.broadcast_to(np.concatenate([bq[order], bk, bv, bo]), (P, QKV + D))
    inv = (f32(1.0) / np.power(f32(10000.0), np.arange(0, HD, 2, dtype=f32) / f32(HD))).astype(f32)
    ang = np.repeat(np.outer(np.arange(T, dtype=f32), inv).astype(f32), 2, axis=1)
    sign = np.tile(np.array([-1.0, 1.0], f32), HD // 2)
    rope = np.stack([np.cos(ang), np.sin(ang) * sign]).astype(f32).reshape(2, TT, P, HD).transpose(2, 0, 1, 3)
    ident = np.eye(P, dtype=f32)
    after = np.triu(np.full((P, P), NEG, f32), 1)
    mask = np.stack([after, after.T], axis=1)
    arrays = {"x_dram": x.reshape(T, D), "w_dram": w, "gate_dram": gates, "qkvo_dram": qkvo, "bias_dram": biases,
              "rope_dram": rope, "ident_dram": ident, "mask_dram": mask}
    arrays = {k: np.ascontiguousarray(a) for k, a in arrays.items()}
    nc = bacc.Bacc("TRN2", target_bir_lowering=False, num_devices=1)
    aps = [nc.dram_tensor(k, a.shape, F32, kind="ExternalInput").ap() for k, a in arrays.items()]
    out = nc.dram_tensor("out_dram", (T, D), F32, kind="ExternalOutput").ap()
    build(nc, *aps, out, stages=stages)
    return nc, arrays, x.shape
```

```python
import concourse.bass as bass
from concourse import mybir
from contextlib import ExitStack

F32, F16, BF16 = mybir.dt.float32, mybir.dt.float16, mybir.dt.bfloat16
ALU, ACT, AX = mybir.AluOpType, mybir.ActivationFunctionType, mybir.AxisListType

P = 128
T, D = 1024, 256
TT = T // P
KC = D // P
NE, FE, FS = 16, 176, 704
TOPK = 4
FEXP = NE * FE
MX = FEXP // P
MT = -(-(FEXP + FS) // P)
FR = FEXP + FS - (MT - 1) * P
assert 2 * FR == P
WC = 3 * D
NG = NE + 1
NC = 2
CH = T // NC
TPC = TT // NC
NH, NKV, HD = 32, 8, 8
GQ = NH // NKV
QW, KW = NH * HD, NKV * HD
QKV = QW + 2 * KW
ROW = 32
GLO = P // ROW
GHI = NKV // GLO
EPS = 1e-5
WS = 64.0
NEG = -1.0e30
SCALE = HD ** -0.5
RING = 3
ORDER = (2, 3, 7, 6, 5, 4, 1, 0)
UH = NH // GHI
AHEAD = 1
RINGED = ("pj", "kx", "q1", "m", "q2", "f1", "f2b", "f3")


def coefficient_spans():
    spans = []
    for m in range(MT):
        f0 = m * P
        if m < MX:
            e = f0 // FE
            cut = min(P, (e + 1) * FE - f0)
            nxt = e + 1
        else:
            e, cut, nxt = NE, P, NE
        if cut == P:
            cut, nxt = P // 2, e
        spans.append([(m, 0, cut, e), (m, cut, P - cut, nxt)])
    return spans


def attention_schedule():
    PE, DVE, ACTE, POOL = range(4)
    streams = [[], [], [], []]
    for t in range(-2, TT + 1):
        streams[1] += [("sp", t)] * (0 <= t < TT) + [("pj", t + 2)] * (t + 2 < TT) + [("kx", t - 1)] * (t >= 1)
    k, late = 0, []
    for i, t in enumerate(ORDER):
        streams[0].append(("q1", i))
        for h in range(NH):
            for kc in range(t // 4 + 1):
                streams[0].append(("m", k, i, h, kc))
                k += 1
            if h % UH == AHEAD - 1 and late:
                streams[0].append(("q2", late.pop()))
            if h % UH == UH - 1:
                u = 2 * i + h // UH
                streams[0].append(("mx", u))
                if u < 2 or u == 2 * TT - 1:
                    streams[0].append(("q2", u))
                else:
                    late.append(u)
    n, last = 0, None
    for i, t in enumerate(ORDER):
        for g in range(GHI):
            for kt in range(t + 1):
                streams[3] += [("st", n, pair, 2 * i + g, g, kt, i) for pair in range(2)]
                if last:
                    streams[3].append(("pv",) + last)
                    if last[3] == ORDER[last[4]]:
                        streams[3].append(("o", last[1]))
                last = (n, 2 * i + g, g, kt, i)
                n += 1
        streams[2] += [("f1", 2 * i)] + [("va", 0)] * (i == TT - 2)
        streams[2] += [("f1", 2 * i + 1), ("f2a", i), ("f2b", i), ("f3", i)]
    streams[3] += [("pv",) + last, ("o", last[1])]

    def work(e):
        kind, t = e[0], e[1]
        if kind == "va":
            return [(DVE, 3.2)], []
        if kind == "pj":
            return [(PE, 1.0), (DVE, 1.2), (POOL, 1.8)], [("sp", t - 2)]
        if kind == "sp":
            return [(ACTE, 0.9), (DVE, 0.7)], [("pj", t)]
        if kind == "kx":
            return [(PE, 0.15), (ACTE, 1.1)], [("sp", t)]
        if kind == "q1":
            return [(PE, 0.5), (ACTE, 1.0)], [("kx", ORDER[t])]
        if kind == "m":
            cols = min(4, ORDER[e[2]] + 1 - 4 * e[4]) * P
            return [(PE, 0.06 + cols / 2400), (DVE, 0.07 + cols / 960)], [("q1", e[2])]
        if kind == "mx":
            return [(DVE, 0.6)], []
        if kind == "q2":
            return [(PE, 0.25), (ACTE, 0.6)], [("mx", t), ("last_st", t - 4)]
        if kind == "st":
            diag = e[5] == ORDER[e[6]]
            return [(PE, 0.9 if diag else 0.45), (ACTE, 0.95)], [("q2", e[3]), ("st", e[1] - 1, e[2])]
        if kind == "pv":
            return [(PE, 1.4)], [("st", t, 1), ("o", e[2] - 1)] + [("pj", e[4])]
        if kind == "o":
            return [(ACTE, 0.55)], [("last_pv", t), ("f1", t - 2)]
        if kind == "f1":
            return [(PE, 0.5), (DVE, 0.9)], [("o", t), ("f2a", t // 2 - 1)]
        if kind == "f2a":
            return [(ACTE, 0.3), (DVE, 0.4)], [("f1", 2 * t + 1)]
        if kind == "f2b":
            return [(PE, 0.25), (ACTE, 0.55)], [("f2a", t)]
        return [(PE, 0.7), (DVE, 0.4)], [("f2b", t)]

    free, done, ring, events, at = [0.0] * 4, {}, [0.0] * RING, [], [0] * 4

    def start(e):
        ops, after = work(e)
        begin = free[ops[0][0]]
        for a in after:
            if a[1] < 0:
                continue
            if a not in done:
                return None
            begin = max(begin, done[a])
        if e[0] in RINGED:
            begin = max(begin, ring[0])
        return begin

    while any(at[i] < len(streams[i]) for i in range(4)):
        ready = [(b, i) for i in range(4) if at[i] < len(streams[i])
                 for b in [start(streams[i][at[i]])] if b is not None]
        begin, i = min(ready)
        e = streams[i][at[i]]
        at[i] += 1
        now = begin
        for engine, cost in work(e)[0]:
            now = max(now, free[engine]) + cost
            free[engine] = now
            now += 0.15
        done[e if e[0] != "st" else e[:3]] = now
        if e[0] == "pv" and e[4] == ORDER[e[5]]:
            done[("last_pv", e[2])] = now
        if e[0] == "st" and e[2] == 1 and e[5] == ORDER[e[6]]:
            done[("last_st", e[3])] = now
        if e[0] in RINGED:
            ring = ring[1:] + [now]
        events.append(e)
    return events


def build(nc, x_in, w_in, gate_in, qkvo_in, bias_in, rope_in, ident_in, mask_in, out):
    ctx = ExitStack()
    with ctx:
        def sb(name, shape, dt):
            return ctx.enter_context(nc.sbuf_tensor(name, shape, dt))

        def sem(name):
            return ctx.enter_context(nc.semaphore(name))

        psum = ctx.enter_context(nc.psum_tensor("psum", [P, 8 * 512], F32))
        bank = [psum[:, 512 * i:512 * (i + 1)] for i in range(8)]
        coef_dram = [nc.dram_tensor(f"coef_dram{f}", (NG, T), F32).ap() for f in range(2)]

        x_res = sb("x_res", [P, TT, D], F32)
        xT = sb("xT", [P, 2, KC, T], F16)
        W_hi = sb("W_hi", [P, MT, WC], F16)
        W_lo = sb("W_lo", [P, MT, WC], F16)
        gate_f = sb("gate_f", [P, KC, NG], F32)
        gate_h = sb("gate_h", [P, 2, KC, NG], F16)
        qkvo_h = sb("qkvo_h", [P, 2, KC, QKV + D], F16)
        bias = sb("bias", [P, QKV + D], F32)
        rope = sb("rope", [P, 2, TT, HD], F32)
        ident = sb("ident", [P, P], F32)
        ident16 = sb("ident16", [P, P], F16)
        identb = sb("identb", [P, P], BF16)
        maskf = sb("maskf", [P, 2, P], F32)
        maskb = sb("maskb", [P, 2, P], BF16)
        w_stage = sb("w_stage", [P, 2, WC], F32)

        R1 = sb("R1", [P, 4096], F32)
        R2 = sb("R2", [P, 4096], F32)
        xn = R1[:, 0:2048].rearrange("p (t d) -> p t d", t=TT)
        x_hl = R1[:, 2048:4096].bitcast(F16).rearrange("p (a t d) -> p a t d", a=2, t=TT)
        v = R1[:, 0:2048].rearrange("p (s c n) -> p s c n", s=2, c=NC)
        hc = R1[:, 2048:3072].rearrange("p (c n) -> p c n", c=NC)
        sg = R1[:, 3072:4096].rearrange("p (c n) -> p c n", c=NC)
        hT = R2[:, 0:2048].bitcast(F16).rearrange("p (a s n) -> p a s n", a=2, s=2)
        C = R2[:, 2048:4096].rearrange("p (s n) -> p s n", s=2)
        qaug = R2[:, :].bitcast(F16).rearrange("p (t h r) -> p t h r", t=TT, r=ROW)
        prob = R1[:, :].rearrange("p (s g n) -> p s g n", s=2, g=GLO)
        kT = sb("kT", [P, NKV, T], F16)
        qkvo_f = kT[:, :, :].rearrange("p g n -> p (g n)").bitcast(F32)[:, 0:KC * (QKV + D)]\
            .rearrange("p (k n) -> p k n", k=KC)
        kaug = sb("kaug", [P, TT, NKV, ROW], F16)
        vals = sb("vals", [P, TT, NKV, 32], F32)
        qkv = sb("qkv", [P, 2, QKV], F32)
        rot_a = sb("rot_a", [P, 2, QW + KW], F32)
        rot_b = sb("rot_b", [P, 2, QW + KW], F32)
        qT1 = sb("qT1", [P, 2, GHI * GQ, P], F16)
        qT2 = sb("qT2", [P, 4, GQ, P], F16)
        m_part = sb("m_part", [P, NH, 2], F32)
        m_row = sb("m_row", [P, UH], F32)
        oT = sb("oT", [P, 2, 512], F32)
        o_rs = sb("o_rs", [P, 2, GQ, GLO], F32)
        o_tok = sb("o_tok", [P, D], F32)
        o_hl = sb("o_hl", [P, 2, D], F16)
        oTT = sb("oTT", [P, 2, KC, P], F16)
        st = sb("st", [P, TT, 6], F32)
        mv = sb("mv", [P, TT, 2], F32)
        sd = sb("sd", [P, TT], F32)
        rs = sb("rs", [P, TT], F32)
        lg = sb("lg", [P, TT, NG], F32)
        mx = sb("mx", [P, TT], F32)
        ex = sb("ex", [P, TT, NG], F32)
        den = sb("den", [P, TT, 2], F32)
        rden = sb("rden", [P, TT, 2], F32)
        pr = sb("pr", [P, TT, NE + TOPK], F32)
        top = sb("top", [P, TT, 8], F32)
        rest = sb("rest", [P, TT, NE + TOPK], F32)
        cf = sb("cf", [P, TT, NG], F32)
        cT = oT[0:NG, :, :].rearrange("p a n -> p (a n)")

        s_x = [sem(f"s_x{t}") for t in range(TT)]
        s_const = sem("s_const")
        s_late = sem("s_late")
        s_qkvo = sem("s_qkvo")
        s_w = [sem(f"s_w{i}") for i in range(2)]
        s_dve = sem("s_dve")
        s_pool = sem("s_pool")
        s_whi = sem("s_whi")
        s_wlo = sem("s_wlo")
        s_ghi = sem("s_ghi")
        s_glo = sem("s_glo")
        s_var = sem("s_var")
        s_sd = sem("s_sd")
        s_xn = sem("s_xn")
        s_xh = sem("s_xh")
        s_xl = [sem(f"s_xl{h}") for h in range(2)]
        s_xps = sem("s_xps")
        s_xT = sem("s_xT")
        s_lg = sem("s_lg")
        s_d = sem("s_d")
        s_ex = sem("s_ex")
        s_cf = sem("s_cf")
        s_cps = sem("s_cps")
        s_cT = sem("s_cT")
        s_cdram = sem("s_cdram")
        s_C = [sem(f"s_C{i}") for i in range(2)]
        s_gu = [sem(f"s_gu{c}") for c in range(NC)]
        s_sg = [sem(f"s_sg{c}") for c in range(NC)]
        s_v = [sem(f"s_v{c}") for c in range(NC)]
        s_hc = [sem(f"s_hc{c}") for c in range(NC)]
        s_hhi = [sem(f"s_hhi{c}") for c in range(NC)]
        s_hlo = [sem(f"s_hlo{c}") for c in range(NC)]
        s_y = [sem(f"s_y{c}") for c in range(NC)]
        s_res = sem("s_res")
        s_ident = sem("s_ident")
        s_out = sem("s_out")
        s_qkvo_h = sem("s_qkvo_h")
        s_qkvo_l = sem("s_qkvo_l")
        s_ready = sem("s_ready")
        s_xb = sem("s_xb")
        s_vals = sem("s_vals")
        s_swap = sem("s_swap")
        s_rot = sem("s_rot")
        s_qkhi = sem("s_qkhi")
        s_qklo = sem("s_qklo")
        s_fill = [sem(f"s_fill{i}") for i in range(RING)]
        s_free = [sem(f"s_free{i}") for i in range(RING)]
        s_m = sem("s_m")
        s_st = sem("s_st")
        s_exp = sem("s_exp")
        s_pv = sem("s_pv")
        s_oT = sem("s_oT")
        s_ohi = sem("s_ohi")
        s_olo = sem("s_olo")
        N_CONST, N_LATE = 2 * 16, 3 * 16
        events = attention_schedule()
        turn = {e: n for n, e in enumerate(e for e in events if e[0] in RINGED)}
        last_m = {2 * e[2] + e[3] // UH: e for e in events if e[0] == "m"}
        ring_bank = [bank[4], bank[5], bank[7]]
        unit_end = {e[2]: e[1] + 1 for e in events if e[0] == "pv"}

        def filled(eng, e):
            eng.wait_ge(s_fill[turn[e] % RING], turn[e] // RING + 1)
            return ring_bank[turn[e] % RING]

        def taken(eng, e):
            eng.wait_ge(s_free[turn[e] % RING], turn[e] // RING + 1)

        def free_of(e):
            return s_free[turn[e] % RING]

        block = ctx.enter_context(nc.Block())

        @block.sync
        def _(sp):
            xv = x_in.rearrange("(t p) d -> t p d", p=P)
            for t in range(TT):
                sp.dma_start(x_res[:, t, :], xv[t]).then_inc(s_x[t], 16)
                if t == TPC - 1:
                    sp.dma_start(ident[:], ident_in).then_inc(s_const, 16)
                    sp.dma_start(gate_f[:], gate_in).then_inc(s_const, 16)
                if t >= TT - 2:
                    sp.dma_start(w_stage[:, t % 2, :], w_in[t % 2]).then_inc(s_w[t % 2], 16)
            sp.dma_start(maskf[:], mask_in).then_inc(s_late, 16)
            sp.dma_start(bias[:], bias_in).then_inc(s_late, 16)
            sp.dma_start(rope[:], rope_in).then_inc(s_late, 16)
            sp.dma_start(qkvo_f, qkvo_in).then_inc(s_qkvo, 16)

            def coefficients(f):
                sp.wait_ge(s_cT, 2 * (f + 1))
                for m, pair in enumerate(coefficient_spans()):
                    M = f * MT + m
                    if m == 2:
                        sp.wait_ge(s_cdram, 16 * (f + 1))
                    if M >= 2:
                        sp.wait_ge(s_hc[0], M - 1)
                        sp.wait_ge(s_hc[1], M - 1)
                    for _, p0, n, e in pair:
                        row = coef_dram[f][e:e + 1, :].to_broadcast([n, T]) if m >= 2 else \
                            cT[e:e + 1, :].unsqueeze(1).to_broadcast([1, n, T])
                        sp.dma_start(C[p0:p0 + n, m % 2, :], row).then_inc(s_C[m % 2], 16)
                    if m == 1:
                        sp.dma_start(coef_dram[f], cT).then_inc(s_cdram, 16)

            coefficients(0)
            coefficients(1)
            ov = out.rearrange("(t p) d -> p t d", p=P)
            for b in range(4):
                sp.wait_ge(s_res, 4 + b + 1)
                sp.dma_start(ov[:, 2 * b:2 * b + 2, :], x_res[:, 2 * b:2 * b + 2, :]).then_inc(s_out, 16)
            sp.wait_ge(s_out, 64)

        @block.gpsimd
        def _(pool):
            def weighted(f, m, j, c):
                M = f * MT + m
                pool.wait_ge(s_v[c], M + 1)
                pool.wait_ge(s_C[j], 32 * (M // 2 + 1) if isinstance(M, int) else 16 * (M - j) + 32)
                if not isinstance(M, int) or M >= 1:
                    pool.wait_ge(s_hlo[c], M)
                nc.gpsimd.tensor_tensor(hc[:, c, :], v[:, j, c, :], C[:, j, c * CH:(c + 1) * CH],
                                        ALU.mult).then_inc(s_hc[c], 1)

            def constants():
                pool.wait_ge(s_qkvo_l, 1)
                nc.gpsimd.memset(kT[:, :, :].rearrange("p g n -> p (g n)").bitcast(F32), 0.0)
                nc.gpsimd.memset(kaug[:], 0.0)
                nc.gpsimd.memset(vals[:], 0.0).then_inc(s_pool, 1)
                pool.wait_ge(s_pool, 1)
                nc.gpsimd.memset(kaug[:, :, :, 24:26], 1.0)
                nc.gpsimd.memset(vals[:, :, :, HD:HD + 1], 1.0).then_inc(s_ready, 1)

            def ffn(f, between=None):
                def step(s, j):
                    for c in range(NC):
                        weighted(f, s - 1, 1 - j, c)
                step(1, 1)
                step(2, 0)
                if between:
                    between()
                step(3, 1)
                with pool.Fori(2, MT // 2 - 1) as i:
                    step(2 * i, 0)
                    step(2 * i + 1, 1)
                step(MT - 2, 0)
                step(MT - 1, 1)
                for c in range(NC):
                    weighted(f, MT - 1, 1, c)

            def low_parts(r):
                for t in range(TPC):
                    pool.wait_ge(s_xh, r * TT + t + 1)
                    nc.gpsimd.tensor_tensor(x_hl[:, 1, t, :], xn[:, t, :], x_hl[:, 0, t, :],
                                            ALU.subtract).then_inc(s_xl[0], 1)

            low_parts(0)
            ffn(0, constants)
            low_parts(1)
            for c in range(NC):
                pool.wait_ge(s_y[c], MT)
            nc.gpsimd.memset(qaug[:, :, :, 24:32], 0.0).then_inc(s_ready, 1)
            for t in range(TT):
                taken(pool, ("pj", t))
                if t >= 2:
                    pool.wait_ge(s_qklo, t - 1)
                cos = rope[:, 0, t, :].unsqueeze(1).to_broadcast([P, NH + NKV, HD])
                ra = rot_a[:, t % 2, :]
                nc.gpsimd.tensor_tensor(ra.rearrange("p (h d) -> p h d", d=HD),
                                        qkv[:, t % 2, 0:QW + KW].rearrange("p (h d) -> p h d", d=HD),
                                        cos, ALU.mult).then_inc(s_pool, 1)
                pool.wait_ge(s_pool, 2 + t)
                pool.wait_ge(s_swap, t + 1)
                nc.gpsimd.tensor_tensor(ra, ra, rot_b[:, t % 2], ALU.add).then_inc(s_rot, 1)
            pool.wait_ge(s_xn, 2 * TT)
            for t in range(TT):
                nc.gpsimd.tensor_tensor(x_res[:, t, :], x_res[:, t, :], bias[:, QKV:QKV + D],
                                        ALU.add).then_inc(s_xb, 1)
            low_parts(2)
            ffn(1)

        @block.scalar
        def _(act):
            def load_weights(m, j):
                if not isinstance(m, int) or m >= 2:
                    act.wait_ge(s_wlo, m - 1)
                src = w_in[m] if isinstance(m, int) else w_in[bass.ds(m, 1), :, :].rearrange("o p n -> p (o n)")
                act.dma_start(w_stage[:, j, :], src).then_inc(s_w[j], 16)

            def weights_high(m, j):
                act.wait_ge(s_w[j], 16 * (m // 2 + 1) if isinstance(m, int) else 8 * (m - j) + 16)
                nc.scalar.activation(W_hi[:, m, :], w_stage[:, j, :], ACT.Copy, scale=WS).then_inc(s_whi, 1)

            def layer_norm(r):
                def deviation(h, tiles=TPC):
                    act.wait_ge(s_var, 2 * r + h + 1)
                    half = slice(h * TPC, h * TPC + tiles)
                    nc.scalar.activation(sd[:, half], mv[:, half, 1], ACT.Sqrt).then_inc(s_sd, 1)

                def high_part(t):
                    act.wait_ge(s_xn, r * TT + t + 1)
                    nc.scalar.activation(x_hl[:, 0, t, :], xn[:, t, :], ACT.Copy).then_inc(s_xh, 1)

                def evacuate(t):
                    act.wait_ge(s_xps, r * TT + t + 1)
                    ps = bank[t % 4][:, 0:256].bitcast(F16).rearrange("p (a k n) -> p a k n", a=2, k=KC)
                    nc.scalar.activation(xT[:, :, :, t * P:(t + 1) * P], ps, ACT.Copy).then_inc(s_xT, 1)

                deviation(0, TT if r == 2 else TPC)
                for t in range(TPC):
                    high_part(t)
                if r == 0:
                    act.wait_ge(s_const, N_CONST)
                    nc.scalar.activation(gate_h[:, 0], gate_f[:], ACT.Copy, scale=WS).then_inc(s_ghi, 1)
                    weights_high(0, 0)
                if r < 2:
                    deviation(1)
                for t in range(TT):
                    evacuate(t)
                    if t + TPC < TT:
                        high_part(t + TPC)

            def silu(f, m, c):
                M = f * MT + m
                act.wait_ge(s_gu[c], M + 1)
                if not isinstance(M, int) or M >= 1:
                    act.wait_ge(s_v[c], M)
                nc.scalar.activation(sg[:, c, :], bank[c][:, :], ACT.Silu, scale=1.0 / WS).then_inc(s_sg[c], 1)

            def silu_last(f, c):
                M = f * MT + MT - 1
                act.wait_ge(s_gu[c], M + 1)
                act.wait_ge(s_v[c], M)
                nc.scalar.activation(sg[0:FR, c, :], bank[c][0:FR, :], ACT.Silu, scale=1.0 / WS).then_inc(s_sg[c], 1)

            def high(f, m, j, c):
                M = f * MT + m
                act.wait_ge(s_hc[c], M + 1)
                if not isinstance(M, int) or M >= 2:
                    act.wait_ge(s_y[c], M - 1)
                nc.scalar.activation(hT[:, 0, j, c * CH:(c + 1) * CH], hc[:, c, :], ACT.Copy).then_inc(s_hhi[c], 1)

            def ffn(f):
                act.wait_ge(s_d, f + 1)
                nc.scalar.activation(ex[:], lg[:], ACT.Exp).then_inc(s_ex, 1)

                def step(s, j):
                    if f == 0 and (not isinstance(s, int) or s + 2 < MT):
                        load_weights(s + 2, j)
                    if f == 0 and (not isinstance(s, int) or s + 1 < MT):
                        weights_high(s + 1, 1 - j)
                    for c in range(NC):
                        silu(f, s, c)
                        if not isinstance(s, int) or s >= 2:
                            high(f, s - 1, 1 - j, c)
                step(0, 0)
                for h in range(2):
                    act.wait_ge(s_cps, 2 * f + h + 1)
                    nc.scalar.activation(cT[:, h * 512:(h + 1) * 512], bank[7 - h][0:NG, :],
                                         ACT.Copy).then_inc(s_cT, 1)
                step(1, 1)
                if f == 0:
                    act.wait_ge(s_qkvo, 16)
                    nc.scalar.activation(qkvo_h[:, 0], qkvo_f, ACT.Copy, scale=WS).then_inc(s_qkvo_h, 1)
                for c in range(NC):
                    high(f, 0, 0, c)
                step(2, 0)
                step(3, 1)
                with act.Fori(2, MT // 2 - 1) as i:
                    step(2 * i, 0)
                    step(2 * i + 1, 1)
                step(MT - 2, 0)
                for c in range(NC):
                    silu_last(f, c)
                    high(f, MT - 2, 0, c)
                for c in range(NC):
                    high(f, MT - 1, 1, c)

            layer_norm(0)
            ffn(0)
            layer_norm(1)

            for e in events:
                kind, t = e[0], e[1]
                if kind == "sp":
                    act.wait_ge(s_rot, t + 1)
                    if t == 0:
                        act.wait_ge(s_ready, 2)
                    q = rot_a[:, t % 2, 0:QW].rearrange("p (h d) -> p h d", d=HD).unsqueeze(2)
                    k = rot_a[:, t % 2, QW:QW + KW].rearrange("p (h d) -> p h d", d=HD).unsqueeze(2)
                    nc.scalar.activation(qaug[:, t].rearrange("p h (a d) -> p h a d", d=HD)[:, :, 0:4:2, :],
                                         q.to_broadcast([P, NH, 2, HD]), ACT.Copy)
                    nc.scalar.activation(kaug[:, t].rearrange("p h (a d) -> p h a d", d=HD)[:, :, 0:2, :],
                                         k.to_broadcast([P, NKV, 2, HD]), ACT.Copy).then_inc(s_qkhi, 1)
                elif kind == "kx":
                    ps = filled(act, e)[:, 0:P].bitcast(F16).rearrange("p (a n) -> p a n", a=GHI)
                    for g in range(GLO):
                        rows = slice(ROW * g, ROW * (g + 1))
                        ins = nc.scalar.activation(kT[rows, g:NKV:GLO, t * P:(t + 1) * P], ps[rows], ACT.Copy)
                    ins.then_inc(free_of(e), 1)
                elif kind == "q1":
                    ps = filled(act, e)
                    nc.scalar.activation(qT1[:, t % 2].rearrange("p a n -> p (a n)"), ps.bitcast(F16),
                                         ACT.Copy).then_inc(free_of(e), 1)
                elif kind == "q2":
                    ps = filled(act, e)[:, 0:GQ * P // 2].bitcast(F16)
                    nc.scalar.activation(qT2[:, t % 4].rearrange("p a n -> p (a n)"), ps,
                                         ACT.Copy).then_inc(free_of(e), 1)
                elif kind == "st":
                    n, pair = e[1], e[2]
                    act.wait_ge(s_st, 2 * n + pair + 1)
                    if n >= 2:
                        act.wait_ge(s_pv, n - 1)
                    nc.scalar.activation(prob[:, n % 2, 2 * pair:2 * pair + 2, :].rearrange("p g n -> p (g n)"),
                                         psum[:, 1024 * pair:1024 * (pair + 1)], ACT.Exp,
                                         scale=SCALE).then_inc(s_exp, 1)
                elif kind == "o":
                    u = t
                    act.wait_ge(s_pv, unit_end[u])
                    if u >= 2:
                        taken(act, ("f1", u - 2))
                    nc.scalar.activation(oT[:, u % 2, :], bank[6], ACT.Copy).then_inc(s_oT, 1)
                elif kind == "f2a":
                    taken(act, ("f1", 2 * t))
                    taken(act, ("f1", 2 * t + 1))
                    nc.scalar.activation(o_hl[:, 0], o_tok[:], ACT.Copy).then_inc(s_ohi, 1)
                elif kind == "f2b":
                    ps = filled(act, e)
                    nc.scalar.activation(oTT[:, :, :, :].rearrange("p a k n -> p (a k n)"),
                                         ps[:, 0:256].bitcast(F16), ACT.Copy).then_inc(free_of(e), 1)
            layer_norm(2)
            ffn(1)

        @block.vector
        def _(dve):
            chain = [0]

            def link(ins):
                chain[0] += 1
                ins.then_inc(s_dve, 1)
                dve.wait_ge(s_dve, chain[0])

            def layer_norm(r):
                def statistics(h):
                    tiles = range(h * TPC, (h + 1) * TPC) if r < 2 else ORDER[-2:]
                    for t in tiles:
                        if r == 0:
                            dve.wait_ge(s_x[t], 16)
                        elif r == 1:
                            dve.wait_ge(s_res, t // 2 + 1)
                        else:
                            taken(dve, ("f3", ORDER.index(t)))
                        ins = nc.vector.bn_stats(st[:, t, :], x_res[:, t, :])
                    link(ins)
                    for t in tiles:
                        ins = nc.vector.bn_aggr(mv[:, t, :], st[:, t, :])
                    link(ins)
                    var = mv[:, h * TPC:(h + 1) * TPC, 1] if r < 2 else mv[:, :, 1]
                    nc.vector.tensor_scalar(var, var, EPS, None, ALU.add).then_inc(s_var, 1)

                def normalise(t):
                    if t == 0 or (t == TPC and r < 2):
                        h = t // TPC
                        dve.wait_ge(s_sd, 2 * r + h + 1)
                        half = slice(t, t + TPC if r < 2 else TT)
                        link(nc.vector.reciprocal(rs[:, half], sd[:, half]))
                    nc.vector.tensor_scalar(xn[:, t, :], x_res[:, t, :], mv[:, t, 0:1], rs[:, t:t + 1],
                                            ALU.subtract, ALU.mult).then_inc(s_xn, 1)

                def low_part(t):
                    dve.wait_ge(s_xh, r * TT + t + 1)
                    nc.vector.tensor_tensor(x_hl[:, 1, t, :], xn[:, t, :], x_hl[:, 0, t, :],
                                            ALU.subtract).then_inc(s_xl[1], 1)

                statistics(0)
                if r == 0:
                    dve.wait_ge(s_const, N_CONST)
                    nc.vector.tensor_copy(ident16[:], ident[:]).then_inc(s_ident, 1)
                for t in range(TPC):
                    normalise(t)
                if r == 1:
                    residual(0, 1)
                if r < 2:
                    statistics(1)
                for t in range(TPC, TT):
                    normalise(t)
                    if t > TPC:
                        low_part(t - 1)
                low_part(TT - 1)

            def residual(f, c):
                dve.wait_ge(s_y[c], (f + 1) * MT)
                for b in (2 * c, 2 * c + 1):
                    xr = x_res[:, 2 * b:2 * b + 2, :]
                    nc.vector.scalar_tensor_tensor(out=xr, in0=bank[4 + b].rearrange("p (t d) -> p t d", t=2),
                                                   scalar=0.5 / WS, in1=xr, op0=ALU.mult,
                                                   op1=ALU.add).then_inc(s_res, 1)

            def router(f):
                dve.wait_ge(s_lg, f + 1)
                link(nc.vector.tensor_scalar(lg[:], bank[6][:, 0:TT * NG].rearrange("p (t e) -> p t e", t=TT),
                                             1.0 / WS, None, ALU.mult))
                link(nc.vector.tensor_reduce(mx[:], lg[:, :, 0:NE], axis=AX.X, op=ALU.max))
                nc.vector.tensor_tensor(lg[:, :, 0:NE], lg[:, :, 0:NE],
                                        mx[:, :].unsqueeze(2).to_broadcast([P, TT, NE]), ALU.subtract)
                nc.vector.tensor_scalar(lg[:, :, NE:NG], lg[:, :, NE:NG], -1.0, None, ALU.mult).then_inc(s_d, 1)
                dve.wait_ge(s_ex, f + 1)
                nc.vector.tensor_reduce(den[:, :, 0:1], ex[:, :, 0:NE], axis=AX.X, op=ALU.add)
                link(nc.vector.tensor_scalar(den[:, :, 1:2], ex[:, :, NE:NG], 1.0, None, ALU.add))
                link(nc.vector.reciprocal(rden[:], den[:]))
                nc.vector.tensor_tensor(pr[:, :, 0:NE], ex[:, :, 0:NE],
                                        rden[:, :, 0:1].to_broadcast([P, TT, NE]), ALU.mult)
                link(nc.vector.tensor_copy(cf[:, :, NE:NG], rden[:, :, 1:2]))
                for t in range(TT):
                    ins = nc.vector.max(top[:, t, :], pr[:, t, :])
                link(ins)
                link(nc.vector.memset(top[:, :, TOPK:8], -1.0))
                for t in range(TT):
                    ins = nc.vector.match_replace(out=rest[:, t, :], in_to_replace=top[:, t, :],
                                                  in_values=pr[:, t, :], imm_value=0.0)
                link(ins)
                nc.vector.tensor_tensor(cf[:, :, 0:NE], pr[:, :, 0:NE], rest[:, :, 0:NE],
                                        ALU.subtract).then_inc(s_cf, 1)

            def weights_low(m, j):
                dve.wait_ge(s_whi, m + 1)
                nc.vector.scalar_tensor_tensor(out=W_lo[:, m, :], in0=w_stage[:, j, :], scalar=WS,
                                               in1=W_hi[:, m, :], op0=ALU.mult,
                                               op1=ALU.subtract).then_inc(s_wlo, 1)

            def gated(f, m, j, c):
                M = f * MT + m
                dve.wait_ge(s_sg[c], M + 1)
                if not isinstance(M, int) or M >= 2:
                    dve.wait_ge(s_hc[c], M - 1)
                nc.vector.scalar_tensor_tensor(out=v[:, j, c, :], in0=bank[2 + c][:, :], scalar=1.0 / WS,
                                               in1=sg[:, c, :], op0=ALU.mult, op1=ALU.mult).then_inc(s_v[c], 1)

            def gated_last(f, c):
                M = f * MT + MT - 1
                dve.wait_ge(s_sg[c], M + 1)
                dve.wait_ge(s_hc[c], M - 1)
                nc.vector.scalar_tensor_tensor(out=v[0:FR, 1, c, :], in0=bank[c][FR:P, :], scalar=1.0 / WS,
                                               in1=sg[0:FR, c, :], op0=ALU.mult, op1=ALU.mult).then_inc(s_v[c], 1)

            def low(f, m, j, c):
                M = f * MT + m
                dve.wait_ge(s_hhi[c], M + 1)
                nc.vector.tensor_tensor(hT[:, 1, j, c * CH:(c + 1) * CH], hc[:, c, :],
                                        hT[:, 0, j, c * CH:(c + 1) * CH], ALU.subtract).then_inc(s_hlo[c], 1)

            def ffn(f):
                router(f)

                def step(s, j):
                    if f == 0 and (not isinstance(s, int) or s + 1 < MT):
                        weights_low(s + 1, 1 - j)
                    for c in range(NC):
                        gated(f, s, j, c)
                        if not isinstance(s, int) or s >= 2:
                            low(f, s - 1, 1 - j, c)
                step(0, 0)
                step(1, 1)
                if f == 0:
                    dve.wait_ge(s_late, N_LATE)
                    nc.vector.tensor_copy(identb[:], ident[:])
                    nc.vector.tensor_copy(maskb[:], maskf[:])
                    dve.wait_ge(s_qkvo_h, 1)
                    nc.vector.scalar_tensor_tensor(out=qkvo_h[:, 1], in0=qkvo_f, scalar=WS, in1=qkvo_h[:, 0],
                                                   op0=ALU.mult, op1=ALU.subtract).then_inc(s_qkvo_l, 1)
                for c in range(NC):
                    low(f, 0, 0, c)
                step(2, 0)
                step(3, 1)
                with dve.Fori(2, MT // 2 - 1) as i:
                    step(2 * i, 0)
                    step(2 * i + 1, 1)
                step(MT - 2, 0)
                for c in range(NC):
                    gated_last(f, c)
                    low(f, MT - 2, 0, c)
                for c in range(NC):
                    low(f, MT - 1, 1, c)
                residual(f, 0)

            nc.vector.memset(pr[:, :, NE:NE + TOPK], -1.0)
            layer_norm(0)
            dve.wait_ge(s_ghi, 1)
            nc.vector.scalar_tensor_tensor(out=gate_h[:, 1], in0=gate_f[:], scalar=WS, in1=gate_h[:, 0],
                                           op0=ALU.mult, op1=ALU.subtract).then_inc(s_glo, 1)
            weights_low(0, 0)
            ffn(0)
            layer_norm(1)

            for e in events:
                kind, t = e[0], e[1]
                if kind == "va":
                    for t in ORDER[:-2]:
                        taken(dve, ("f3", ORDER.index(t)))
                        ins = nc.vector.bn_stats(st[:, t, :], x_res[:, t, :])
                    link(ins)
                    for t in ORDER[:-2]:
                        nc.vector.bn_aggr(mv[:, t, :], st[:, t, :])
                elif kind == "pj":
                    ps = filled(dve, e)
                    if t >= 2:
                        dve.wait_ge(s_rot, t - 1)
                    nc.vector.scalar_tensor_tensor(out=qkv[:, t % 2, :], in0=ps[:, 0:QKV], scalar=1.0 / WS,
                                                   in1=bias[:, 0:QKV], op0=ALU.mult,
                                                   op1=ALU.add).then_inc(free_of(e), 1)
                    taken(dve, e)
                    if t == 0:
                        dve.wait_ge(s_ready, 1)
                    nc.vector.tensor_copy(vals[:, t, :, 0:HD],
                                          qkv[:, t % 2, QW + KW:QKV].rearrange("p (h d) -> p h d", d=HD)
                                          ).then_inc(s_vals, 1)
                    x = qkv[:, t % 2, 0:QW + KW].rearrange("p (h n e) -> p h n e", n=HD // 2, e=2)
                    sin = rope[:, 1, t, :].rearrange("p (n e) -> p n e", e=2).unsqueeze(1)\
                        .to_broadcast([P, NH + NKV, HD // 2, 2])
                    nc.vector.tensor_tensor(rot_b[:, t % 2].rearrange("p (h n e) -> p h n e", n=HD // 2, e=2),
                                            x[:, :, :, ::-1], sin, ALU.mult).then_inc(s_swap, 1)
                elif kind == "sp":
                    dve.wait_ge(s_qkhi, t + 1)
                    q = rot_a[:, t % 2, 0:QW].rearrange("p (h d) -> p h d", d=HD)
                    k = rot_a[:, t % 2, QW:QW + KW].rearrange("p (h d) -> p h d", d=HD)
                    nc.vector.tensor_tensor(qaug[:, t, :, HD:2 * HD], q, qaug[:, t, :, 0:HD], ALU.subtract)
                    nc.vector.tensor_tensor(kaug[:, t, :, 2 * HD:3 * HD], k, kaug[:, t, :, 0:HD],
                                            ALU.subtract).then_inc(s_qklo, 1)
                elif kind == "m":
                    _, k, i, h, kc = e
                    t = ORDER[i]
                    ps = filled(dve, e)
                    n = min(4, t + 1 - 4 * kc) * P
                    u = 2 * i + h // UH
                    if (h % UH, kc) == (0, 0) and u >= 2:
                        dve.wait_ge(s_m, u - 1)
                    nc.vector.tensor_reduce(m_part[:, h, kc:kc + 1], ps[:, 0:n], axis=AX.X,
                                            op=ALU.max).then_inc(free_of(e), 1)
                elif kind == "mx":
                    u, t, h = t, ORDER[t // 2], slice(UH * (t % 2), UH * (t % 2 + 1))
                    taken(dve, last_m[u])
                    m_all = m_part[:, h, 0]
                    if t >= 4:
                        if u >= 1:
                            dve.wait_ge(s_m, u)
                        link(nc.vector.tensor_tensor(m_row[:], m_part[:, h, 0], m_part[:, h, 1], ALU.max))
                        m_all = m_row[:]
                    link(nc.vector.tensor_scalar(qaug[:, t, h, 24], m_all, -1.0, None, ALU.mult))
                    nc.vector.scalar_tensor_tensor(out=qaug[:, t, h, 25], in0=m_all, scalar=-1.0,
                                                   in1=qaug[:, t, h, 24], op0=ALU.mult,
                                                   op1=ALU.subtract).then_inc(s_m, 1)
                elif kind == "f1":
                    u = t
                    ps = filled(dve, e).rearrange("p (j g r) -> p j g r", j=GQ, g=GLO)
                    if u >= 2:
                        taken(dve, ("f1", u - 2))
                    link(nc.vector.reciprocal(o_rs[:, u % 2], ps[:, :, :, HD]))
                    if u % 2 == 0 and u >= 2:
                        dve.wait_ge(s_olo, u // 2)
                    o = o_tok[:, (u % 2) * P:(u % 2 + 1) * P].rearrange("p (g j d) -> p j g d", g=GLO, j=GQ)
                    nc.vector.tensor_tensor(o, ps[:, :, :, 0:HD],
                                            o_rs[:, u % 2].unsqueeze(3).to_broadcast([P, GQ, GLO, HD]),
                                            ALU.mult).then_inc(free_of(e), 1)
                elif kind == "f2a":
                    dve.wait_ge(s_ohi, t + 1)
                    nc.vector.tensor_tensor(o_hl[:, 1], o_tok[:], o_hl[:, 0], ALU.subtract).then_inc(s_olo, 1)
                elif kind == "f3":
                    ps = filled(dve, e)
                    t = ORDER[t]
                    dve.wait_ge(s_xb, t + 1)
                    nc.vector.scalar_tensor_tensor(out=x_res[:, t, :], in0=ps[:, 0:D], scalar=1.0 / WS,
                                                   in1=x_res[:, t, :], op0=ALU.mult,
                                                   op1=ALU.add).then_inc(free_of(e), 1)
            layer_norm(2)
            ffn(1)
            residual(1, 1)

        @block.tensor
        def _(pe):
            def split_product(o, stat, mov, k_parts, first=True, last=True, **kw):
                n = 0
                for k in range(k_parts):
                    for a, b in ((0, 0), (0, 1), (1, 0)):
                        ins = nc.tensor.matmul(o, stat(a, k), mov(b, k), start=first and n == 0,
                                               stop=last and n == 3 * k_parts - 1, **kw)
                        n += 1
                return ins

            def layer_norm(r, tiles=range(TT)):
                for t in tiles:
                    pe.wait_ge(s_xl[t // TPC], r * TPC + t % TPC + 1)
                    if t >= 4:
                        pe.wait_ge(s_xT, r * TT + t - 3)
                    ps = bank[t % 4][:, 0:256].bitcast(F16)
                    for a in range(2):
                        for k in range(KC):
                            q = a * KC + k
                            ins = nc.tensor.transpose(ps[:, q * P:(q + 1) * P],
                                                      x_hl[:, a, t, k * P:(k + 1) * P], ident16[:])
                    ins.then_inc(s_xps, 1)

            def gate_up(f, m, c):
                M = f * MT + m
                if f == 0:
                    pe.wait_ge(s_wlo, m + 1)
                if not isinstance(M, int) or M >= 1:
                    pe.wait_ge(s_v[c], M)
                parts = (W_hi, W_lo)
                for u in range(1 if isinstance(m, int) and m == MT - 1 else 2):
                    ins = split_product(
                        bank[2 * u + c][:, :],
                        lambda a, k: parts[a][:, m, (2 * u + k) * P:(2 * u + k + 1) * P],
                        lambda b, k: xT[:, b, k, c * CH:(c + 1) * CH], KC)
                ins.then_inc(s_gu[c], 1)

            def down(f, m, j, c, first=False, last=False):
                M = f * MT + m
                pe.wait_ge(s_hlo[c], M + 1)
                parts = (W_hi, W_lo)
                for t in range(c * TPC, (c + 1) * TPC):
                    o = bank[4 + t // 2][:, (t % 2) * D:(t % 2 + 1) * D]
                    ins = split_product(o, lambda a, k: hT[:, a, j, t * P:(t + 1) * P],
                                        lambda b, k: parts[b][:, m, 2 * D:3 * D], 1,
                                        first=first and t % 2 == 0, last=last, skip_group_check=True)
                ins.then_inc(s_y[c], 1)

            def ffn(f):
                for t in range(TT):
                    pe.wait_ge(s_xT, f * 2 * TT + t + 1)
                    if f == 0 and t == 0:
                        pe.wait_ge(s_glo, 1)
                    ins = split_product(bank[6][:, t * NG:(t + 1) * NG],
                                        lambda a, k: xT[:, a, k, t * P:(t + 1) * P],
                                        lambda b, k: gate_h[:, b, k, :], KC)
                ins.then_inc(s_lg, 1)

                def step(s, j, **kw):
                    for c in range(NC):
                        gate_up(f, s, c)
                        if not isinstance(s, int) or s >= 2:
                            down(f, s - 2, j, c, **kw)
                step(0, 0)
                pe.wait_ge(s_cf, f + 1)
                for t in range(TT):
                    ins = nc.tensor.transpose(bank[7 - t // 4][0:NG, (t % 4) * P:(t % 4 + 1) * P],
                                              cf[:, t, :], ident[:])
                    if t % 4 == 3:
                        ins.then_inc(s_cps, 1)
                step(1, 1)
                for c in range(NC):
                    gate_up(f, 2, c)
                    if c == 0:
                        pe.wait_ge(s_cT, 2 * (f + 1))
                    down(f, 0, 0, c, first=True)
                step(3, 1)
                with pe.Fori(2, MT // 2 - 1) as i:
                    step(2 * i, 0)
                    step(2 * i + 1, 1)
                step(MT - 2, 0)
                step(MT - 1, 1)
                for c in range(NC):
                    down(f, MT - 2, 0, c)
                    down(f, MT - 1, 1, c, last=True)

            pe.wait_ge(s_ident, 1)
            layer_norm(0)
            ffn(0)
            def project(t, to):
                pe.wait_ge(s_xT, TT + t + 1)
                return split_product(to[:, 0:QKV], lambda a, k: xT[:, a, k, t * P:(t + 1) * P],
                                     lambda b, k: qkvo_h[:, b, k, 0:QKV], KC)

            layer_norm(1, range(TPC))
            for t in range(2):
                project(t, ring_bank[t]).then_inc(s_fill[t], 1)
            layer_norm(1, range(TPC, TT))

            for e in events[2:]:
                kind, t = e[0], e[1]
                if kind in RINGED:
                    k = turn[e]
                    out_bank, full = ring_bank[k % RING], s_fill[k % RING]
                    if k >= RING:
                        pe.wait_ge(s_free[k % RING], k // RING)
                if kind == "pj":
                    project(t, out_bank).then_inc(full, 1)
                elif kind == "kx":
                    pe.wait_ge(s_qklo, t + 1)
                    ps = out_bank[:, 0:P].bitcast(F16)
                    for a in range(GHI):
                        ins = nc.tensor.transpose(ps[:, a * P:(a + 1) * P],
                                                  kaug[:, t, GLO * a:GLO * (a + 1), :].rearrange("p h r -> p (h r)"),
                                                  ident16[:])
                    ins.then_inc(full, 1)
                elif kind in ("q1", "q2"):
                    if kind == "q1":
                        t, groups = ORDER[t], range(GHI * GQ)
                        taken(pe, ("kx", t))
                    else:
                        pe.wait_ge(s_m, t + 1)
                        t, groups = ORDER[t // 2], range(GQ * (t % 2), GQ * (t % 2 + 1))
                    ps = out_bank.bitcast(F16)
                    for k, q in enumerate(groups):
                        ins = nc.tensor.transpose(ps[:, k * P:(k + 1) * P],
                                                  qaug[:, t, GLO * q:GLO * (q + 1), :].rearrange("p h r -> p (h r)"),
                                                  ident16[:])
                    ins.then_inc(full, 1)
                elif kind == "m":
                    _, k, i, h, kc = e
                    t = ORDER[i]
                    if (h, kc) == (0, 0):
                        taken(pe, ("q1", i))
                    g = h // (GQ * GLO) * GLO + h % GLO
                    n = min(4, t + 1 - 4 * kc) * P
                    diag = kc == t // 4
                    if diag:
                        nc.tensor.matmul(out_bank[:, n - P:n], identb[:], maskb[:, 0, :],
                                         start=True, stop=False, skip_group_check=True)
                    nc.tensor.matmul(out_bank[:, 0:n], qT1[:, i % 2, h // GLO, :],
                                     kT[:, g, kc * 512:kc * 512 + n], start=not diag, stop=True,
                                     skip_group_check=diag).then_inc(full, 1)
                elif kind == "st":
                    _, n, pair, u, gh, kt, i = e
                    t = ORDER[i]
                    if n >= 1:
                        pe.wait_ge(s_exp, 2 * (n - 1) + pair + 1)
                    if kt == 0 and pair == 0:
                        taken(pe, ("q2", u))
                    for gl in (2 * pair, 2 * pair + 1):
                        ins = nc.tensor.matmul(bank[gl], kT[:, gh * GLO + gl, kt * P:(kt + 1) * P],
                                               qT2[:, u % 4, :, :], start=True, stop=kt != t)
                        if kt == t:
                            ins = nc.tensor.matmul(bank[gl].rearrange("p (j n) -> p j n", j=GQ), identb[:],
                                                   maskb[:, 1, :].unsqueeze(1).to_broadcast([P, GQ, P]),
                                                   start=False, stop=True)
                    ins.then_inc(s_st, 1)
                elif kind == "pv":
                    _, n, u, gh, kt, i = e
                    t = ORDER[i]
                    pe.wait_ge(s_exp, 2 * n + 2)
                    if kt == 0:
                        pe.wait_ge(s_vals, t + 1)
                    if kt == 0 and u >= 1:
                        pe.wait_ge(s_oT, u)
                    for gl in range(GLO):
                        ins = nc.tensor.matmul(bank[6][32 * gl:32 * (gl + 1), :], vals[:, kt, gh * GLO + gl, :],
                                               prob[:, n % 2, gl, :], start=kt == 0, stop=kt == t)
                    ins.then_inc(s_pv, 1)
                elif kind == "f1":
                    u = t
                    pe.wait_ge(s_oT, u + 1)
                    for j in range(GQ):
                        ins = nc.tensor.transpose(out_bank[:, j * P:(j + 1) * P], oT[:, u % 2, j * P:(j + 1) * P],
                                                  ident[:])
                    ins.then_inc(full, 1)
                elif kind == "f2b":
                    pe.wait_ge(s_olo, t + 1)
                    ps = out_bank[:, 0:256].bitcast(F16)
                    for a in range(2):
                        for k in range(KC):
                            q = a * KC + k
                            ins = nc.tensor.transpose(ps[:, q * P:(q + 1) * P], o_hl[:, a, k * P:(k + 1) * P],
                                                      ident16[:])
                    ins.then_inc(full, 1)
                elif kind == "f3":
                    taken(pe, ("f2b", t))
                    split_product(out_bank[:, 0:D], lambda a, k: oTT[:, a, k, :],
                                  lambda b, k: qkvo_h[:, b, k, QKV:QKV + D], KC).then_inc(full, 1)
            layer_norm(2)
            ffn(1)


def kernel(L0_attn_x, L0_attn_Wq, L0_attn_bq, L0_attn_Wk, L0_attn_bk, L0_attn_Wv, L0_attn_bv, L0_attn_Wo,
           L0_attn_bo, L0_ffn_gate_w, L0_ffn_sgate_w, L0_ffn_w13, L0_ffn_w2, L0_ffn_shared_gate_up_w,
           L0_ffn_shared_down_w):
    import numpy as np
    import concourse.bacc as bacc
    from concourse.bass_utils import run_bass_kernel_spmd

    nc, arrays, shape = program_and_arrays(np, bacc, L0_attn_x, L0_attn_Wq, L0_attn_bq, L0_attn_Wk, L0_attn_bk,
                                           L0_attn_Wv, L0_attn_bv, L0_attn_Wo, L0_attn_bo, L0_ffn_gate_w,
                                           L0_ffn_sgate_w, L0_ffn_w13, L0_ffn_w2, L0_ffn_shared_gate_up_w,
                                           L0_ffn_shared_down_w)
    r = run_bass_kernel_spmd(nc, [arrays], core_ids=[0])
    return r.results[0]["out_dram"].reshape(shape)


def program_and_arrays(np, bacc, x, Wq, bq, Wk, bk, Wv, bv, Wo, bo, gate_w, sgate_w, w13, w2, sgu, sdn):
    f32 = np.float32
    x, Wq, bq, Wk, bk, Wv, bv, Wo, bo, gate_w, sgate_w, w13, w2, sgu, sdn = (
        np.asarray(a) for a in (x, Wq, bq, Wk, bk, Wv, bv, Wo, bo, gate_w, sgate_w, w13, w2, sgu, sdn))

    def lhs(rows):
        full = np.zeros((MT * P, D), f32)
        full[:len(rows)] = rows
        return full.reshape(MT, P, KC, P).transpose(0, 3, 2, 1).reshape(MT, P, D)

    gate_rows = np.concatenate([w13[:, :FE].reshape(FEXP, D), sgu[:FS]])
    up_rows = np.concatenate([w13[:, FE:].reshape(FEXP, D), sgu[FS:]])
    down = np.zeros((MT * P, D), f32)
    down[:FEXP + FS] = np.concatenate([w2.transpose(0, 2, 1).reshape(FEXP, D), sdn.T])
    w = np.concatenate([lhs(gate_rows), lhs(up_rows), down.reshape(MT, P, D)], axis=2)
    last_g, last_u = (w[MT - 1, :, a * D:(a + 1) * D].reshape(P, KC, P) for a in range(2))
    last_g[:, :, FR:] = last_u[:, :, :FR]
    last_u[:] = 0.0
    gates = np.concatenate([gate_w, sgate_w]).T.reshape(KC, P, NG).transpose(1, 0, 2)
    order = np.arange(QW).reshape(GHI, GLO, GQ, HD).transpose(0, 2, 1, 3).reshape(-1)
    qkvo = np.concatenate([Wq[:, order], Wk, Wv, Wo], axis=1).reshape(KC, P, QKV + D).transpose(1, 0, 2)
    biases = np.broadcast_to(np.concatenate([bq[order], bk, bv, bo]), (P, QKV + D))
    inv = (f32(1.0) / np.power(f32(10000.0), np.arange(0, HD, 2, dtype=f32) / f32(HD))).astype(f32)
    ang = np.repeat(np.outer(np.arange(T, dtype=f32), inv).astype(f32), 2, axis=1)
    sign = np.tile(np.array([-1.0, 1.0], f32), HD // 2)
    rope = np.stack([np.cos(ang), np.sin(ang) * sign]).astype(f32).reshape(2, TT, P, HD).transpose(2, 0, 1, 3)
    ident = np.eye(P, dtype=f32)
    after = np.triu(np.full((P, P), NEG, f32), 1)
    mask = np.stack([after, after.T], axis=1)
    arrays = {"x_dram": x.reshape(T, D), "w_dram": w, "gate_dram": gates, "qkvo_dram": qkvo, "bias_dram": biases,
              "rope_dram": rope, "ident_dram": ident, "mask_dram": mask}
    arrays = {k: np.ascontiguousarray(a) for k, a in arrays.items()}
    nc = bacc.Bacc("TRN2", target_bir_lowering=False, num_devices=1)
    aps = [nc.dram_tensor(k, a.shape, F32, kind="ExternalInput").ap() for k, a in arrays.items()]
    out = nc.dram_tensor("out_dram", (T, D), F32, kind="ExternalOutput").ap()
    build(nc, *aps, out)
    return nc, arrays, x.shape
```
